# Optimizing a Trainium2 kernel written in Bass

```python
import numpy as np
import jax
import jax.numpy as jnp

def _softmax(x, axis=-1):
    return jax.nn.softmax(x, axis=axis)

def _gelu(x):
    return jax.nn.gelu(x, approximate=True)

def _silu(x):
    return jax.nn.silu(x)

def _sigmoid(x):
    return jax.nn.sigmoid(x)

def _layernorm(x, axis=-1, eps=1e-05):
    m = jnp.mean(x, axis=axis, keepdims=True)
    v = jnp.var(x, axis=axis, keepdims=True)
    return (x - m) / jnp.sqrt(v + eps)

def _scatter_add(tgt, idx, src, axis=0):
    return tgt.at[idx].add(src)

def _segment_sum(src, seg, n):
    return jax.ops.segment_sum(src, seg, n)
kernel_name = 'mk_sandwich_d1_jaxref_r8_fa8151'

def setup_inputs(seed: int=0):
    np.random.seed(seed)
    _w = jnp.asarray

    def _L0_attn_setup():
        import jax, jax.numpy as jnp
        import numpy as np
        B, S, D_IN, D_H = (4, 256, 128, 128)
        key = jax.random.key(seed)
        ks = jax.random.split(key, 7)
        s_in = 1.0 / np.sqrt(D_IN)
        x = jax.random.normal(ks[0], (B, S, D_IN), dtype=jnp.float32)
        Wq = jax.random.uniform(ks[1], (D_IN, D_H), jnp.float32, -s_in, s_in)
        Wk = jax.random.uniform(ks[2], (D_IN, D_H), jnp.float32, -s_in, s_in)
        Wv = jax.random.uniform(ks[3], (D_IN, D_H), jnp.float32, -s_in, s_in)
        bq = jax.random.uniform(ks[4], (D_H,), jnp.float32, -s_in, s_in)
        bk = jax.random.uniform(ks[5], (D_H,), jnp.float32, -s_in, s_in)
        bv = jax.random.uniform(ks[6], (D_H,), jnp.float32, -s_in, s_in)
        return {'x': x, 'Wq': Wq, 'bq': bq, 'Wk': Wk, 'bk': bk, 'Wv': Wv, 'bv': bv}
    _L0_attn_in = _L0_attn_setup()

    def _L0_ffn_setup():
        import jax, jax.numpy as jnp
        import numpy as np
        B, S, D, H, M, E, K = (8, 256, 128, 256, 64, 8, 2)
        EH = H // 2

        def _layernorm(x, g, b, eps=1e-05):
            mu = jnp.mean(x, axis=-1, keepdims=True)
            var = jnp.var(x, axis=-1, keepdims=True)
            return (x - mu) * jax.lax.rsqrt(var + eps) * g + b
        key = jax.random.key(seed)
        ks = jax.random.split(key, 16)
        sc = lambda *shape: 1.0 / np.sqrt(shape[0])
        return {'inputs_embeds': jax.random.normal(ks[0], (B, S, D), jnp.float32), 'W_enc': jax.random.normal(ks[1], (D, H), jnp.float32) * sc(D), 'b_enc': jnp.zeros((H,), jnp.float32), 'W_s2c': jax.random.normal(ks[2], (H, M), jnp.float32) * sc(H), 'b_s2c': jnp.zeros((M,), jnp.float32), 'Wr': jax.random.normal(ks[3], (M, E), jnp.float32) * sc(M), 'br': jnp.zeros((E,), jnp.float32), 'W1': jax.random.normal(ks[4], (E, M, EH), jnp.float32) * sc(M), 'b1': jnp.zeros((E, EH), jnp.float32), 'W2': jax.random.normal(ks[5], (E, EH, M), jnp.float32) * sc(EH), 'b2': jnp.zeros((E, M), jnp.float32), 'W_c2s': jax.random.normal(ks[6], (M, H), jnp.float32) * sc(M), 'b_c2s': jnp.zeros((H,), jnp.float32), 'W_dec': jax.random.normal(ks[7], (H, D), jnp.float32) * sc(H), 'b_dec': jnp.zeros((D,), jnp.float32), 'ln_g': jnp.ones((D,), jnp.float32), 'ln_b': jnp.zeros((D,), jnp.float32)}
    _L0_ffn_in = _L0_ffn_setup()
    _d = {'L0_attn_x': _L0_attn_in['x'], 'L0_attn_Wq': _L0_attn_in['Wq'], 'L0_attn_bq': _L0_attn_in['bq'], 'L0_attn_Wk': _L0_attn_in['Wk'], 'L0_attn_bk': _L0_attn_in['bk'], 'L0_attn_Wv': _L0_attn_in['Wv'], 'L0_attn_bv': _L0_attn_in['bv'], 'L0_ffn_W_enc': _L0_ffn_in['W_enc'], 'L0_ffn_b_enc': _L0_ffn_in['b_enc'], 'L0_ffn_W_s2c': _L0_ffn_in['W_s2c'], 'L0_ffn_b_s2c': _L0_ffn_in['b_s2c'], 'L0_ffn_Wr': _L0_ffn_in['Wr'], 'L0_ffn_br': _L0_ffn_in['br'], 'L0_ffn_W1': _L0_ffn_in['W1'], 'L0_ffn_b1': _L0_ffn_in['b1'], 'L0_ffn_W2': _L0_ffn_in['W2'], 'L0_ffn_b2': _L0_ffn_in['b2'], 'L0_ffn_W_c2s': _L0_ffn_in['W_c2s'], 'L0_ffn_b_c2s': _L0_ffn_in['b_c2s'], 'L0_ffn_W_dec': _L0_ffn_in['W_dec'], 'L0_ffn_b_dec': _L0_ffn_in['b_dec'], 'L0_ffn_ln_g': _L0_ffn_in['ln_g'], 'L0_ffn_ln_b': _L0_ffn_in['ln_b']}
    _x0 = _d['L0_attn_x']
    _d['L0_attn_x'] = jax.random.normal(jax.random.fold_in(jax.random.key(seed), 1), (4, 512, 128), dtype=_x0.dtype)
    del _x0
    return _d

def reference(L0_attn_x, L0_attn_Wq, L0_attn_bq, L0_attn_Wk, L0_attn_bk, L0_attn_Wv, L0_attn_bv, L0_ffn_W_enc, L0_ffn_b_enc, L0_ffn_W_s2c, L0_ffn_b_s2c, L0_ffn_Wr, L0_ffn_br, L0_ffn_W1, L0_ffn_b1, L0_ffn_W2, L0_ffn_b2, L0_ffn_W_c2s, L0_ffn_b_c2s, L0_ffn_W_dec, L0_ffn_b_dec, L0_ffn_ln_g, L0_ffn_ln_b):

    def _L0_attn_ref(x, Wq, bq, Wk, bk, Wv, bv):
        import jax, jax.numpy as jnp
        import numpy as np
        B, S, D_IN, D_H = (4, 256, 128, 128)
        q = jnp.einsum('bsd,dh->bsh', x, Wq) + bq
        k = jnp.einsum('bsd,dh->bsh', x, Wk) + bk
        v = jnp.einsum('bsd,dh->bsh', x, Wv) + bv
        scale = jnp.asarray(D_H, x.dtype) ** 0.5
        scores = jnp.einsum('bqh,bkh->bqk', q, k) / scale
        probs = jax.nn.softmax(scores, axis=-1)
        return jnp.einsum('bqk,bkh->bqh', probs, v)

    def _L0_ffn_ref(inputs_embeds, W_enc, b_enc, W_s2c, b_s2c, Wr, br, W1, b1, W2, b2, W_c2s, b_c2s, W_dec, b_dec, ln_g, ln_b):
        import jax, jax.numpy as jnp
        import numpy as np
        B, S, D, H, M, E, K = (8, 256, 128, 256, 64, 8, 2)
        EH = H // 2

        def _layernorm(x, g, b, eps=1e-05):
            mu = jnp.mean(x, axis=-1, keepdims=True)
            var = jnp.var(x, axis=-1, keepdims=True)
            return (x - mu) * jax.lax.rsqrt(var + eps) * g + b
        b, s, d = inputs_embeds.shape
        spikes_enc = jax.nn.sigmoid(inputs_embeds @ W_enc + b_enc)
        flat = spikes_enc.reshape(b * s, -1)
        cont = flat @ W_s2c + b_s2c
        probs = jax.nn.softmax(cont @ Wr + br, axis=-1)
        topk_w, topk_idx = jax.lax.top_k(probs, K)
        topk_w = topk_w / jnp.sum(topk_w, axis=-1, keepdims=True)
        gate = jnp.sum(jax.nn.one_hot(topk_idx, E, dtype=cont.dtype) * topk_w[..., None], axis=1)
        h = jax.nn.relu(jnp.einsum('tm,emh->eth', cont, W1) + b1[:, None, :])
        y = jnp.einsum('eth,ehm->etm', h, W2) + b2[:, None, :]
        expert_out = jnp.einsum('etm,te->tm', y, gate)
        spikes_moe = jax.nn.sigmoid(expert_out @ W_c2s + b_c2s)
        spikes_moe = spikes_moe.reshape(b, s, -1)
        decoded = spikes_moe @ W_dec + b_dec
        return _layernorm(decoded, ln_g, ln_b)
    x = L0_attn_x
    x = x + _layernorm(_L0_attn_ref(_layernorm(x, axis=-1), L0_attn_Wq, L0_attn_bq, L0_attn_Wk, L0_attn_bk, L0_attn_Wv, L0_attn_bv), axis=-1)
    x = x + _layernorm(_L0_ffn_ref(_layernorm(x, axis=-1), L0_ffn_W_enc, L0_ffn_b_enc, L0_ffn_W_s2c, L0_ffn_b_s2c, L0_ffn_Wr, L0_ffn_br, L0_ffn_W1, L0_ffn_b1, L0_ffn_W2, L0_ffn_b2, L0_ffn_W_c2s, L0_ffn_b_c2s, L0_ffn_W_dec, L0_ffn_b_dec, L0_ffn_ln_g, L0_ffn_ln_b), axis=-1)
    return x

_drawn_inputs = setup_inputs


def setup_inputs(seed=0):
    import zlib

    import numpy as np

    out = dict(_drawn_inputs(seed))
    spreads = {'L0_ffn_b_enc': (0.0, 0.8),
     'L0_ffn_b_s2c': (0.0, 0.1),
     'L0_ffn_br': (0.0, 0.1),
     'L0_ffn_b1': (0.0, 0.63),
     'L0_ffn_b2': (0.0, 0.498),
     'L0_ffn_b_c2s': (0.0, 0.274),
     'L0_ffn_b_dec': (0.0, 0.1),
     'L0_ffn_ln_g': (1.0, 0.2),
     'L0_ffn_ln_b': (0.0, 0.1)}
    factors = {'L0_attn_bq': 3.444, 'L0_attn_bk': 64.0}
    for name, (base, spread) in spreads.items():
        noise = np.random.default_rng([zlib.crc32(name.encode()), seed]).standard_normal(out[name].shape)
        drawn = base * np.exp(spread * noise) if base else spread * noise
        out[name] = jnp.asarray(drawn.astype(out[name].dtype))
    for name, factor in factors.items():
        out[name] = (out[name] * factor).astype(out[name].dtype)
    return out
```

```python
from contextlib import ExitStack

import concourse.bass as bass
from concourse import mybir

ALU = mybir.AluOpType
ACT = mybir.ActivationFunctionType
AX_X = mybir.AxisListType.X
F32 = mybir.dt.float32
F32R = mybir.dt.float32r
BF16 = mybir.dt.bfloat16
U32 = mybir.dt.uint32

P = 128
EPS = 1e-5


def attention_moe_block(
    nc: bass.Bass,
    x, Wq, bq, Wk, bk, Wv, bv,
    W_enc, b_enc, W_s2c, b_s2c, Wr, br, W1, b1, W2, b2,
    W_c2s, b_c2s, W_dec, b_dec, ln_g, ln_b,
    out,
):
    B, S, D = x.shape
    H = W_enc.shape[1]
    M = W_s2c.shape[1]
    E = Wr.shape[1]
    EH = W1.shape[2]
    T = S // P
    HC = H // P
    assert D == P and EH == P and M == 64 and E == 8 and T * D == 512 and E * M == 512
    SCALE = float(D) ** -0.5

    R_Q, R_K, R_ENC, R_C2S, R_B1 = 0, 1, 2, 2 + HC, 2 + 2 * HC
    R_S2C = R_B1 + E
    ROWS = R_S2C + 1

    x_dram = x.rearrange("b (p t) d -> b p t d", t=T)
    out_dram = out.rearrange("b (p t) d -> b p t d", t=T)

    with ExitStack() as ctx:
        def sb(name, shape, dt=F32):
            return ctx.enter_context(nc.sbuf_tensor(name, shape, dt))

        def psum(name):
            return ctx.enter_context(nc.psum_tensor(name, [P, 512], F32))

        def sem(name):
            return ctx.enter_context(nc.semaphore(name))

        ident = sb("ident", [P, P])
        ones = sb("ones", [P, P])
        ones_bf = sb("ones_bf", [P, P], BF16)
        expert_no = sb("expert_no", [P, E])
        minus_half = sb("minus_half", [P, T])
        wq = sb("wq", [P, D])
        wk = sb("wk", [P, D])
        wv = sb("wv", [P, D])
        bv_all = sb("bv_all", [P, D])
        bias_rows = sb("bias_rows", [ROWS, P])
        bias_cols = sb("bias_cols", [P, ROWS])
        bias_half = sb("bias_half", [P, 2 * HC])
        bq_scaled = sb("bq_scaled", [P, 1])
        w_enc = sb("w_enc", [P, H])
        w_s2c_raw = sb("w_s2c_raw", [P, HC, M])
        w_s2c = sb("w_s2c", [P, HC, 2, M])
        b_cont = sb("b_cont", [P, 1])
        w_r = sb("w_r", [M, E])
        br_all = sb("br_all", [P, E])
        w1_raw = sb("w1_raw", [P, E, EH])
        w1_hi = sb("w1_hi", [P, E, EH], F32R)
        w1_lo = sb("w1_lo", [P, E, EH], F32R)
        w2 = sb("w2", [P, E, M])
        b2_row = sb("b2_row", [P, E * M])
        b2_rest = sb("b2_rest", [P, E * M])
        b2_hi = sb("b2_hi", [P, E * M], BF16)
        b2_mid = sb("b2_mid", [P, E * M], BF16)
        b2_stack = sb("b2_stack", [P, E * M], BF16)
        w_c2s_raw = sb("w_c2s_raw", [P, H])
        w_c2s_hi = sb("w_c2s_hi", [P, H], F32R)
        w_c2s_lo = sb("w_c2s_lo", [P, H], F32R)
        w_dec_raw = sb("w_dec_raw", [P, HC, D])
        w_dec = sb("w_dec", [P, HC, D])
        b_dec_row = sb("b_dec_row", [1, D])
        b_dec_sum = sb("b_dec_sum", [P, D])
        b_dec_rest = sb("b_dec_rest", [P, D])
        b_dec_hi = sb("b_dec_hi", [P, D], BF16)
        b_dec_mid = sb("b_dec_mid", [P, D], BF16)
        b_dec_stack = sb("b_dec_stack", [P, D], BF16)
        g_all = sb("g_all", [P, D])
        b_all = sb("b_all", [P, D])

        x_in = sb("x_in", [P, B, T, D])
        x_mid = sb("x_mid", [P, B, T, D])
        x_out = sb("x_out", [P, B, T, D])
        xn = sb("xn", [P, 2, T, D])
        xnT = sb("xnT", [P, 2, S])
        qT = sb("qT", [P, 2, S])
        kT = sb("kT", [P, 2, S])
        v = sb("v", [P, 2, T, D])
        neg_max = sb("neg_max", [P, 2, T])
        prob_sum = sb("prob_sum", [P, 2, T])
        probs = sb("probs", [P, 2, T, S])
        probsT = sb("probsT", [P, 2, T, T, P])
        attn = sb("attn", [P, 2, T, D])
        hn = sb("hn", [P, 2, T, D])
        hT = sb("hT", [P, 2, S])
        spikes = sb("spikes", [P, 2, HC, S])
        cont = sb("cont", [P, 2, S])
        cont_parts = sb("cont_parts", [P, 2, S], F32R)
        logits = sb("logits", [P, 2, T, E])
        top = sb("top", [P, 2, T, 8])
        top_no = sb("top_no", [P, 2, T, 8], U32)
        top_diff = sb("top_diff", [P, 2, T])
        e2 = sb("e2", [P, 2, T])
        e_sum = sb("e_sum", [P, 2, T])
        w_first = sb("w_first", [P, 2, T])
        w_second = sb("w_second", [P, 2, T])
        pick1 = sb("pick1", [P, 2, T, E])
        pick2 = sb("pick2", [P, 2, T, E])
        gate = sb("gate", [P, 2, T, E])
        hidden = sb("hidden", [P, E, S])
        gated = sb("gated", [P, 2, E, M])
        moe = sb("moe", [P, 2, T, 2, M])
        moe_parts = sb("moe_parts", [P, 2, S], F32R)
        spikes2 = sb("spikes2", [P, 2, HC, S])
        z1 = sb("z1", [P, 2, T, D])
        z = sb("z", [P, 2, T, D])
        zn = sb("zn", [P, 2, T, D])

        LN_X, LN_ATT, LN_MID, LN_DEC, LN_Z = range(5)
        stats = sb("stats", [P, 5, 2, T, 6])
        mean_var = sb("mean_var", [P, 5, 2, T, 2])
        eps_term = sb("eps_term", [P, 2, T])
        var_eps = sb("var_eps", [P, 5, 2, T])
        rstd = sb("rstd", [P, 5, 2, T])

        ps_s = [psum("ps_s0"), psum("ps_s1")]
        ps_t = psum("ps_t")
        ps_a = psum("ps_a")
        ps_o = psum("ps_o")
        ring = [psum("ps_f0"), psum("ps_f1"), psum("ps_f2")]
        F_HT, F_ENC, F_CONT, F_LOGIT, F_H = 0, 1, 1 + HC, 2 + HC, 3 + HC
        F_Y = F_H + E
        F_MT = F_Y + T
        F_C2S = F_MT + 1
        F_DEC = F_C2S + HC
        assert (F_DEC + 1) % 3 == 0

        def slot(product):
            return ring[product % 3]

        d_x = [sem(f"d_x{b}") for b in range(B)]
        d_qkv = sem("d_qkv")
        d_rows = sem("d_rows")
        d_enc = sem("d_enc")
        d_s2c = sem("d_s2c")
        d_router = sem("d_router")
        d_w1 = sem("d_w1")
        d_w2 = sem("d_w2")
        d_b2 = sem("d_b2")
        d_c2s = sem("d_c2s")
        d_dec = sem("d_dec")
        d_ln = sem("d_ln")
        d_out = sem("d_out")

        g_zero = sem("g_zero")
        g_const = sem("g_const")
        g_s2c = sem("g_s2c")
        g_dec = sem("g_dec")
        g_zero_rows = sem("g_zero_rows")
        g_eps = [sem(f"g_eps{n}") for n in range(5)]
        g_rstd = [sem(f"g_rstd{n}") for n in range(5)]

        pe_bias = sem("pe_bias")
        pe_bcont = sem("pe_bcont")
        pe_bdec = sem("pe_bdec")
        pe_xnT = sem("pe_xnT")
        pe_q = sem("pe_q")
        pe_k = sem("pe_k")
        pe_v = sem("pe_v")
        pe_s = sem("pe_s")
        pe_pT = sem("pe_pT")
        pe_o = sem("pe_o")
        pe_hT = sem("pe_hT")
        pe_enc = sem("pe_enc")
        pe_cont = sem("pe_cont")
        pe_logit = sem("pe_logit")
        pe_h = sem("pe_h")
        pe_y = sem("pe_y")
        pe_moeT = sem("pe_moeT")
        pe_c2s = sem("pe_c2s")
        pe_dec = sem("pe_dec")

        a_xnT = sem("a_xnT")
        a_q = sem("a_q")
        a_k = sem("a_k")
        a_exp = sem("a_exp")
        a_pT = sem("a_pT")
        a_hT = sem("a_hT")
        a_enc = sem("a_enc")
        a_cont = sem("a_cont")
        a_e2 = sem("a_e2")
        a_h = sem("a_h")
        a_c2s = sem("a_c2s")

        v_bias = sem("v_bias")
        v_bias2 = sem("v_bias2")
        v_bcont = sem("v_bcont")
        v_w1 = sem("v_w1")
        v_c2s = sem("v_c2s")
        v_b2 = sem("v_b2")
        v_bdec = sem("v_bdec")
        v_stats = [sem(f"v_stats{n}") for n in range(5)]
        v_mv = [sem(f"v_mv{n}") for n in range(5)]
        v_xn = sem("v_xn")
        v_v = sem("v_v")
        v_max = sem("v_max")
        v_epst = sem("v_epst")
        v_attn = sem("v_attn")
        v_mid = sem("v_mid")
        v_hn = sem("v_hn")
        v_hi = sem("v_hi")
        v_cont = sem("v_cont")
        v_logit = sem("v_logit")
        v_top = sem("v_top")
        v_topno = sem("v_topno")
        v_diff = sem("v_diff")
        v_gate = sem("v_gate")
        v_gated = sem("v_gated")
        v_moe = sem("v_moe")
        v_mhi = sem("v_mhi")
        v_mparts = sem("v_mparts")
        v_z1 = sem("v_z1")
        v_z = sem("v_z")
        v_zn = sem("v_zn")
        v_out = sem("v_out")

        block = ctx.enter_context(nc.Block())

        @block.sync
        def _(sp):
            for b in range(B):
                sp.dma_start(x_in[:, b], x_dram[b]).then_inc(d_x[b], 16)
                if b == 0:
                    sp.dma_start(wk[:, :], Wk).then_inc(d_qkv, 16)
                    sp.dma_start(wv[:, :], Wv).then_inc(d_qkv, 16)
            sp.dma_start(w_s2c_raw[:, :, :], W_s2c.rearrange("(c p) m -> p c m", p=P)).then_inc(d_s2c, 16)
            for half in range(2):
                sp.dma_start(w1_raw[half * M:(half + 1) * M], W1.rearrange("e m h -> m e h")).then_inc(d_w1, 16)
            sp.dma_start(w2[:, :, :], W2.rearrange("e h m -> h e m")).then_inc(d_w2, 16)
            sp.dma_start(w_dec_raw[:, :, :], W_dec.rearrange("(c p) d -> p c d", p=P)).then_inc(d_dec, 16)
            sp.dma_start(b_dec_row[:, :], b_dec.rearrange("(a d) -> a d", a=1)).then_inc(d_dec, 16)
            for half in range(2):
                sp.dma_start(w_c2s_raw[half * M:(half + 1) * M], W_c2s).then_inc(d_c2s, 16)
            for b in range(B):
                sp.wait_ge(v_out, b + 1)
                sp.dma_start(out_dram[b], x_out[:, b]).then_inc(d_out, 16)
            sp.wait_ge(d_out, 16 * B)

        @block.gpsimd
        def _(pool):
            nc.gpsimd.memset(ident[:, :], 0.0).then_inc(g_zero, 1)
            nc.gpsimd.memset(minus_half[:, :], -0.5).then_inc(g_const, 1)
            pool.wait_ge(g_zero, 1)
            nc.gpsimd.affine_select(out=ident[:, :], in_=ident[:, :], compare_op=ALU.not_equal, fill=1.0, base=0,
                                    pattern=[[-1, P]], channel_multiplier=1).then_inc(g_const, 1)

            def inverse_std(n, b):
                pool.wait_ge(v_mv[n], T * (b + 1))
                variance = mean_var[:, n, b % 2, :, 1]
                if n == LN_ATT:
                    pool.wait_ge(v_epst, b + 1)
                    nc.gpsimd.tensor_tensor(var_eps[:, n, b % 2], variance, eps_term[:, b % 2], ALU.add).then_inc(
                        g_eps[n], 1)
                else:
                    nc.gpsimd.tensor_scalar(var_eps[:, n, b % 2], variance, EPS, None, ALU.add).then_inc(g_eps[n], 1)
                pool.wait_ge(g_eps[n], b + 1)
                nc.gpsimd.tensor_tensor(rstd[:, n, b % 2], var_eps[:, n, b % 2], minus_half[:, :], ALU.pow).then_inc(
                    g_rstd[n], 1)

            nc.gpsimd.memset(b_dec_stack[:, :], 0.0).then_inc(g_zero_rows, 1)
            nc.gpsimd.memset(b2_stack[:, :], 0.0).then_inc(g_zero_rows, 1)
            nc.gpsimd.memset(b2_row[:, :], 0.0).then_inc(g_zero_rows, 1)
            pool.wait_ge(g_zero_rows, 3)
            for row in (0, 32, 64):
                pool.dma_start(b2_row[row:row + 1, :], b2.rearrange("(a e) m -> a (e m)", a=1)).then_inc(d_b2, 16)
            inverse_std(LN_X, 0)
            nc.gpsimd.memset(ones[:, :], 1.0).then_inc(g_const, 1)
            nc.gpsimd.memset(ones_bf[:, :], 1.0).then_inc(g_const, 1)
            for e in range(E):
                nc.gpsimd.memset(expert_no[:, e:e + 1], float(e)).then_inc(g_const, 1)
            pool.wait_ge(d_s2c, 16)
            for half in range(2):
                nc.gpsimd.tensor_scalar(w_s2c[:, :, half], w_s2c_raw[:, :, :], 0.5, None, ALU.mult).then_inc(g_s2c, 1)
            inverse_std(LN_X, 1)
            pool.wait_ge(d_dec, 32)
            nc.gpsimd.tensor_scalar(w_dec[:, :, :], w_dec_raw[:, :, :], 0.5, None, ALU.mult).then_inc(g_dec, 1)
            inverse_std(LN_ATT, 0)
            inverse_std(LN_MID, 0)
            for b in range(B):
                if b >= 1:
                    inverse_std(LN_DEC, b - 1)
                    inverse_std(LN_Z, b - 1)
                if b + 2 < B:
                    inverse_std(LN_X, b + 2)
                if b + 1 < B:
                    inverse_std(LN_ATT, b + 1)
                    inverse_std(LN_MID, b + 1)
            inverse_std(LN_DEC, B - 1)
            inverse_std(LN_Z, B - 1)

        @block.scalar
        def _(act):
            act.dma_start(wq[:, :], Wq).then_inc(d_qkv, 16)
            for row, vec in ((R_Q, bq), (R_K, bk)):
                act.dma_start(bias_rows[row:row + 1, :], vec.rearrange("(a d) -> a d", a=1)).then_inc(d_rows, 16)
            for row, vec in ((R_ENC, b_enc), (R_C2S, b_c2s)):
                act.dma_start(bias_rows[row:row + HC, :], vec.rearrange("(a d) -> a d", a=HC)).then_inc(d_rows, 16)
            act.dma_start(bias_rows[R_B1:R_B1 + E, :], b1).then_inc(d_rows, 16)
            for half in range(2):
                act.dma_start(bias_rows[R_S2C:R_S2C + 1, half * M:(half + 1) * M],
                              b_s2c.rearrange("(a d) -> a d", a=1)).then_inc(d_rows, 16)
            act.dma_start(bv_all[:, :], bv.partition_broadcast(P)).then_inc(d_qkv, 16)
            act.dma_start(w_enc[:, :], W_enc).then_inc(d_enc, 16)
            act.dma_start(w_r[:, :], Wr).then_inc(d_router, 16)
            act.dma_start(br_all[:, :], br.partition_broadcast(P)).then_inc(d_router, 16)
            act.dma_start(g_all[:, :], ln_g.partition_broadcast(P)).then_inc(d_ln, 16)
            act.dma_start(b_all[:, :], ln_b.partition_broadcast(P)).then_inc(d_ln, 16)

            def xnT_out(b):
                act.wait_ge(pe_xnT, b + 1)
                nc.scalar.activation(xnT[:, b % 2], ps_a[:, :], ACT.Identity).then_inc(a_xnT, 1)

            def q_out(b):
                act.wait_ge(pe_q, b + 1)
                nc.scalar.activation(qT[:, b % 2], ps_a[:, :], ACT.Identity, bias=bq_scaled[:, :],
                                     scale=SCALE).then_inc(a_q, 1)

            def k_out(b):
                act.wait_ge(pe_k, b + 1)
                nc.scalar.activation(kT[:, b % 2], ps_a[:, :], ACT.Identity,
                                     bias=bias_cols[:, R_K:R_K + 1]).then_inc(a_k, 1)

            def exps(b, t):
                act.wait_ge(v_max, T * b + t + 1)
                nc.scalar.activation(probs[:, b % 2, t], ps_s[t % 2][:, :], ACT.Exp, bias=neg_max[:, b % 2, t:t + 1],
                                     accum_out=prob_sum[:, b % 2, t:t + 1]).then_inc(a_exp, 1)

            def pT_out(b, t):
                act.wait_ge(pe_pT, T * b + t + 1)
                nc.scalar.activation(probsT[:, b % 2, t], ps_t[:, :].rearrange("p (k q) -> p k q", k=T),
                                     ACT.Identity).then_inc(a_pT, 1)

            def hT_out(b):
                act.wait_ge(pe_hT, b + 1)
                nc.scalar.activation(hT[:, b % 2], slot(F_HT)[:, :], ACT.Identity).then_inc(a_hT, 1)

            def encode(b, c):
                act.wait_ge(pe_enc, HC * b + c + 1)
                nc.scalar.activation(spikes[:, b % 2, c], slot(F_ENC + c)[:, :], ACT.Tanh,
                                     bias=bias_half[:, c:c + 1], scale=0.5).then_inc(a_enc, 1)

            def cont_out(b):
                act.wait_ge(pe_cont, b + 1)
                if b == 0:
                    act.wait_ge(v_bcont, 1)
                nc.scalar.activation(cont[:, b % 2], slot(F_CONT)[:, :], ACT.Identity,
                                     bias=b_cont[:, :]).then_inc(a_cont, 1)

            def second_exp(b):
                act.wait_ge(v_diff, b + 1)
                nc.scalar.activation(e2[:, b % 2], top_diff[:, b % 2], ACT.Exp).then_inc(a_e2, 1)

            def relu(b, e):
                act.wait_ge(pe_h, E * b + e + 1)
                if e == 0 and b >= 1:
                    act.wait_ge(pe_y, T * b)
                nc.scalar.activation(hidden[:, e], slot(F_H + e)[:, :], ACT.Relu,
                                     bias=bias_cols[:, R_B1 + e:R_B1 + e + 1]).then_inc(a_h, 1)

            def spike(b, c):
                act.wait_ge(pe_c2s, HC * b + c + 1)
                nc.scalar.activation(spikes2[:, b % 2, c], slot(F_C2S + c)[:, :], ACT.Tanh,
                                     bias=bias_half[:, HC + c:HC + c + 1], scale=0.5).then_inc(a_c2s, 1)

            xnT_out(0)
            act.wait_ge(v_bias2, 3)
            q_out(0)
            k_out(0)
            exps(0, 0)
            xnT_out(1)
            pT_out(0, 0)
            exps(0, 1)
            q_out(1)
            pT_out(0, 1)
            exps(0, 2)
            k_out(1)
            pT_out(0, 2)
            exps(0, 3)
            pT_out(0, 3)
            for b in range(B):
                more, more2 = b + 1 < B, b + 2 < B
                hT_out(b)
                encode(b, 0)
                if more:
                    exps(b + 1, 0)
                encode(b, 1)
                cont_out(b)
                if more:
                    exps(b + 1, 1)
                    pT_out(b + 1, 0)
                relu(b, 0)
                relu(b, 1)
                second_exp(b)
                relu(b, 2)
                relu(b, 3)
                if more:
                    exps(b + 1, 2)
                    pT_out(b + 1, 1)
                relu(b, 4)
                relu(b, 5)
                if more:
                    exps(b + 1, 3)
                relu(b, 6)
                relu(b, 7)
                if more:
                    pT_out(b + 1, 2)
                    pT_out(b + 1, 3)
                if more2:
                    xnT_out(b + 2)
                    q_out(b + 2)
                    k_out(b + 2)
                for c in range(HC):
                    spike(b, c)

        @block.tensor
        def _(pe):
            def turn_x(b):
                pe.wait_ge(v_xn, T * (b + 1))
                if b == 0:
                    pe.wait_ge(g_const, 2)
                else:
                    pe.wait_ge(v_v, b)
                for t in range(T):
                    mm = nc.tensor.transpose(ps_a[:, t * P:(t + 1) * P], xn[:, b % 2, t], ident[:, :])
                mm.then_inc(pe_xnT, 1)

            def project_q(b):
                pe.wait_ge(a_xnT, b + 1)
                if b == 0:
                    pe.wait_ge(d_qkv, 64)
                nc.tensor.matmul(ps_a[:, :], wq[:, :], xnT[:, b % 2], start=True, stop=True).then_inc(pe_q, 1)

            def project_k(b):
                pe.wait_ge(a_q, b + 1)
                nc.tensor.matmul(ps_a[:, :], wk[:, :], xnT[:, b % 2], start=True, stop=True).then_inc(pe_k, 1)

            def project_v(b):
                pe.wait_ge(a_k, b + 1)
                for t in range(T):
                    mm = nc.tensor.matmul(ps_a[:, t * P:(t + 1) * P], xnT[:, b % 2, t * P:(t + 1) * P], wv[:, :],
                                          start=True, stop=True)
                mm.then_inc(pe_v, 1)

            def scores(b, t):
                if t == 0:
                    pe.wait_ge(a_k, b + 1)
                if T * b + t >= 2:
                    pe.wait_ge(a_exp, T * b + t - 1)
                nc.tensor.matmul(ps_s[t % 2][:, :], qT[:, b % 2, t * P:(t + 1) * P], kT[:, b % 2],
                                 start=True, stop=True).then_inc(pe_s, 1)

            def turn_probs(b, t):
                pe.wait_ge(a_exp, T * b + t + 1)
                if T * b + t >= 1:
                    pe.wait_ge(a_pT, T * b + t)
                for k in range(T):
                    mm = nc.tensor.transpose(ps_t[:, k * P:(k + 1) * P], probs[:, b % 2, t, k * P:(k + 1) * P],
                                             ident[:, :])
                mm.then_inc(pe_pT, 1)

            def attend(b, t):
                pe.wait_ge(a_pT, T * b + t + 1)
                if t == 0:
                    pe.wait_ge(v_v, b + 1)
                    if b >= 1:
                        pe.wait_ge(v_attn, T * b)
                for k in range(T):
                    mm = nc.tensor.matmul(ps_o[:, t * P:(t + 1) * P], probsT[:, b % 2, t, k], v[:, b % 2, k],
                                          start=(k == 0), stop=(k == T - 1))
                if t == T - 1:
                    mm.then_inc(pe_o, 1)

            def turn_h(b):
                pe.wait_ge(v_hn, T * (b + 1))
                if b >= 1:
                    pe.wait_ge(a_c2s, HC * b - 1)
                for t in range(T):
                    mm = nc.tensor.transpose(slot(F_HT)[:, t * P:(t + 1) * P], hn[:, b % 2, t], ident[:, :])
                mm.then_inc(pe_hT, 1)

            def encode(b, c):
                pe.wait_ge(a_hT, b + 1)
                if b == 0:
                    pe.wait_ge(d_enc, 16)
                elif c == 0:
                    pe.wait_ge(a_c2s, HC * b)
                else:
                    pe.wait_ge(v_z1, T * b)
                nc.tensor.matmul(slot(F_ENC + c)[:, :], w_enc[:, c * P:(c + 1) * P], hT[:, b % 2],
                                 start=True, stop=True).then_inc(pe_enc, 1)

            def to_cont(b):
                pe.wait_ge(a_enc, HC * (b + 1))
                for c in range(HC):
                    mm = nc.tensor.matmul(slot(F_CONT)[:, :], w_s2c[:, c], spikes[:, b % 2, c],
                                          start=(c == 0), stop=(c == HC - 1))
                mm.then_inc(pe_cont, 1)

            def route(b):
                pe.wait_ge(a_cont, b + 1)
                if b == 0:
                    pe.wait_ge(d_router, 32)
                for t in range(T):
                    mm = nc.tensor.matmul(slot(F_LOGIT)[:, t * E:(t + 1) * E], cont[0:M, b % 2, t * P:(t + 1) * P],
                                          w_r[:, :], start=True, stop=True)
                mm.then_inc(pe_logit, 1)

            def hidden_units(b, e):
                if e == 0:
                    pe.wait_ge(v_cont, b + 1)
                    if b == 0:
                        pe.wait_ge(v_w1, 2)
                if e == 1:
                    pe.wait_ge(a_cont, b + 1)
                if e == 2:
                    pe.wait_ge(v_logit, b + 1)
                if e >= 3:
                    pe.wait_ge(a_h, E * b + e - 2)
                nc.tensor.matmul(slot(F_H + e)[:, :], w1_hi[:, e], cont_parts[:, b % 2], start=True, stop=False)
                nc.tensor.matmul(slot(F_H + e)[:, :], w1_lo[:, e], cont_parts[:, b % 2], start=False,
                                 stop=True).then_inc(pe_h, 1)

            def expert_out(b, t):
                if t == 0:
                    pe.wait_ge(a_h, E * (b + 1))
                    if b == 0:
                        pe.wait_ge(d_w2, 16)
                        pe.wait_ge(v_b2, 8)
                if t == T - 1:
                    pe.wait_ge(v_gated, T * b + 1)
                y = slot(F_Y + t)
                nc.tensor.matmul(y[:, :], ones_bf[:, :], b2_stack[:, :], start=True, stop=False)
                for e in range(E):
                    mm = nc.tensor.matmul(y[:, e * M:(e + 1) * M], hidden[:, e, t * P:(t + 1) * P], w2[:, e],
                                          start=False, stop=(e == E - 1))
                mm.then_inc(pe_y, 1)

            def turn_moe(b):
                pe.wait_ge(v_moe, 2 * T * (b + 1))
                for t in range(T):
                    mm = nc.tensor.transpose(slot(F_MT)[:, t * P:(t + 1) * P],
                                             moe[:, b % 2, t].rearrange("p a m -> p (a m)"), ident[:, :])
                mm.then_inc(pe_moeT, 1)

            def to_spikes(b, c):
                pe.wait_ge(v_mparts, b + 1)
                if b == 0:
                    pe.wait_ge(v_c2s, 2)
                nc.tensor.matmul(slot(F_C2S + c)[:, :], w_c2s_hi[:, c * P:(c + 1) * P], moe_parts[:, b % 2],
                                 start=True, stop=False)
                nc.tensor.matmul(slot(F_C2S + c)[:, :], w_c2s_lo[:, c * P:(c + 1) * P], moe_parts[:, b % 2],
                                 start=False, stop=True).then_inc(pe_c2s, 1)

            def decode(b):
                pe.wait_ge(a_c2s, HC * (b + 1))
                if b == 0:
                    pe.wait_ge(v_bdec, 9)
                for t in range(T):
                    d = slot(F_DEC)[:, t * P:(t + 1) * P]
                    nc.tensor.matmul(d, ones_bf[:, :], b_dec_stack[:, :], start=True, stop=False)
                    for c in range(HC):
                        mm = nc.tensor.matmul(d, spikes2[:, b % 2, c, t * P:(t + 1) * P], w_dec[:, c],
                                              start=False, stop=(c == HC - 1))
                mm.then_inc(pe_dec, 1)

            pe.wait_ge(d_rows, 16 * 7)
            pe.wait_ge(g_const, 2)
            nc.tensor.transpose(ps_t[:, 0:ROWS], bias_rows[:, :], ident[0:ROWS, 0:ROWS]).then_inc(pe_bias, 1)
            turn_x(0)
            project_q(0)
            project_k(0)
            project_v(0)
            pe.wait_ge(g_s2c, 2)
            pe.wait_ge(g_const, 4)
            for c in range(HC):
                mm = nc.tensor.matmul(ps_o[:, 0:1], w_s2c[:, c], ones[:, 0:1], start=(c == 0), stop=(c == HC - 1))
            mm.then_inc(pe_bcont, 1)
            pe.wait_ge(v_bias, 1)
            scores(0, 0)
            scores(0, 1)
            turn_x(1)
            turn_probs(0, 0)
            scores(0, 2)
            project_q(1)
            pe.wait_ge(v_bcont, 1)
            attend(0, 0)
            turn_probs(0, 1)
            scores(0, 3)
            project_k(1)
            attend(0, 1)
            turn_probs(0, 2)
            project_v(1)
            attend(0, 2)
            turn_probs(0, 3)
            attend(0, 3)
            pe.wait_ge(g_dec, 1)
            for c in range(HC):
                nc.tensor.matmul(ps_t[:, 0:D], ones[:, :], w_dec[:, c], start=(c == 0), stop=False)
            nc.tensor.matmul(ps_t[:, 0:D], ones[0:1, :], b_dec_row[:, :], start=False, stop=True).then_inc(pe_bdec, 1)
            pe.wait_ge(v_bdec, 2)
            for b in range(B):
                n, m = b + 1, b + 2
                more, more2 = n < B, m < B
                turn_h(b)
                if more:
                    scores(n, 0)
                encode(b, 0)
                encode(b, 1)
                if more:
                    scores(n, 1)
                to_cont(b)
                if more:
                    turn_probs(n, 0)
                route(b)
                hidden_units(b, 0)
                hidden_units(b, 1)
                if more:
                    attend(n, 0)
                hidden_units(b, 2)
                if more:
                    scores(n, 2)
                hidden_units(b, 3)
                if more:
                    turn_probs(n, 1)
                hidden_units(b, 4)
                hidden_units(b, 5)
                if more:
                    attend(n, 1)
                    scores(n, 3)
                hidden_units(b, 6)
                hidden_units(b, 7)
                if more:
                    turn_probs(n, 2)
                expert_out(b, 0)
                if more:
                    attend(n, 2)
                    turn_probs(n, 3)
                expert_out(b, 1)
                if more2:
                    turn_x(m)
                if more:
                    attend(n, 3)
                expert_out(b, 2)
                if more2:
                    project_q(m)
                expert_out(b, 3)
                if more2:
                    project_k(m)
                turn_moe(b)
                if more2:
                    project_v(m)
                for c in range(HC):
                    to_spikes(b, c)
                decode(b)

        @block.vector
        def _(dve):
            def statistics(n, b, source):
                for t in range(T):
                    nc.vector.bn_stats(stats[:, n, b % 2, t], source(t)).then_inc(v_stats[n], 1)
                for t in range(T):
                    dve.wait_ge(v_stats[n], T * b + t + 1)
                    nc.vector.bn_aggr(mean_var[:, n, b % 2, t], stats[:, n, b % 2, t]).then_inc(v_mv[n], 1)

            def mean(n, b, t):
                return mean_var[:, n, b % 2, t, 0:1]

            def inv(n, b, t):
                return rstd[:, n, b % 2, t:t + 1]

            def x_stats(b):
                dve.wait_ge(d_x[b], 16)
                statistics(LN_X, b, lambda t: x_in[:, b, t])

            def x_norm(b):
                dve.wait_ge(g_rstd[LN_X], b + 1)
                for t in range(T):
                    nc.vector.tensor_scalar(xn[:, b % 2, t], x_in[:, b, t], mean(LN_X, b, t), inv(LN_X, b, t),
                                            ALU.subtract, ALU.mult).then_inc(v_xn, 1)

            def v_out_(b):
                dve.wait_ge(pe_v, b + 1)
                nc.vector.tensor_tensor(v[:, b % 2], ps_a[:, :].rearrange("p (t d) -> p t d", t=T),
                                        bv_all[:, :].unsqueeze(1).to_broadcast([P, T, D]), ALU.add).then_inc(v_v, 1)

            def row_max(b, t):
                dve.wait_ge(pe_s, T * b + t + 1)
                nc.vector.tensor_reduce(neg_max[:, b % 2, t:t + 1], ps_s[t % 2][:, :], AX_X, ALU.max,
                                        negate=True).then_inc(v_max, 1)

            def attn_stats(b):
                dve.wait_ge(a_exp, T * (b + 1))
                nc.vector.scalar_tensor_tensor(eps_term[:, b % 2], prob_sum[:, b % 2], EPS, prob_sum[:, b % 2],
                                               ALU.mult, ALU.mult).then_inc(v_epst, 1)
                dve.wait_ge(pe_o, b + 1)
                statistics(LN_ATT, b, lambda t: ps_o[:, t * P:(t + 1) * P])

            def attn_norm(b):
                dve.wait_ge(g_rstd[LN_ATT], b + 1)
                for t in range(T):
                    nc.vector.tensor_scalar(attn[:, b % 2, t], ps_o[:, t * P:(t + 1) * P], mean(LN_ATT, b, t),
                                            inv(LN_ATT, b, t), ALU.subtract, ALU.mult).then_inc(v_attn, 1)
                dve.wait_ge(v_attn, T * (b + 1))
                nc.vector.tensor_tensor(x_mid[:, b], attn[:, b % 2], x_in[:, b], ALU.add).then_inc(v_mid, 1)

            def mid_stats(b):
                dve.wait_ge(v_mid, b + 1)
                statistics(LN_MID, b, lambda t: x_mid[:, b, t])

            def mid_norm(b):
                dve.wait_ge(g_rstd[LN_MID], b + 1)
                for t in range(T):
                    nc.vector.tensor_scalar(hn[:, b % 2, t], x_mid[:, b, t], mean(LN_MID, b, t), inv(LN_MID, b, t),
                                            ALU.subtract, ALU.mult).then_inc(v_hn, 1)

            def split_cont(b):
                dve.wait_ge(a_cont, b + 1)
                nc.vector.tensor_copy(cont_parts[:, b % 2], cont[:, b % 2]).then_inc(v_hi, 1)
                dve.wait_ge(v_hi, b + 1)
                nc.vector.tensor_tensor(cont_parts[M:P, b % 2], cont[M:P, b % 2],
                                        cont_parts[M:P, b % 2].bitcast(F32), ALU.subtract).then_inc(v_cont, 1)

            def router_top(b):
                i = b % 2
                dve.wait_ge(pe_logit, b + 1)
                nc.vector.tensor_tensor(logits[:, i], slot(F_LOGIT)[:, 0:T * E].rearrange("p (t e) -> p t e", t=T),
                                        br_all[:, :].unsqueeze(1).to_broadcast([P, T, E]), ALU.add).then_inc(v_logit, 1)
                dve.wait_ge(v_logit, b + 1)
                for t in range(T):
                    nc.vector.max(top[:, i, t], logits[:, i, t]).then_inc(v_top, 1)
                for t in range(T):
                    dve.wait_ge(v_top, T * b + t + 1)
                    nc.vector.max_index(top_no[:, i, t], top[:, i, t], logits[:, i, t]).then_inc(v_topno, 1)
                nc.vector.tensor_tensor(top_diff[:, i], top[:, i, :, 1], top[:, i, :, 0], ALU.subtract).then_inc(v_diff, 1)

            def router_gates(b):
                i = b % 2

                def wide(w):
                    return w[:, i].unsqueeze(2).to_broadcast([P, T, E])

                count = 9 * b
                dve.wait_ge(v_topno, T * (b + 1))
                for pick, j in ((pick1, 0), (pick2, 1)):
                    nc.vector.tensor_tensor(pick[:, i], expert_no[:, :].unsqueeze(1).to_broadcast([P, T, E]),
                                            top_no[:, i, :, j:j + 1].to_broadcast([P, T, E]),
                                            ALU.is_equal).then_inc(v_gate, 1)
                dve.wait_ge(a_e2, b + 1)
                nc.vector.tensor_scalar(e_sum[:, i], e2[:, i], 1.0, None, ALU.add).then_inc(v_gate, 1)
                dve.wait_ge(v_gate, count + 3)
                nc.vector.reciprocal(w_first[:, i], e_sum[:, i]).then_inc(v_gate, 1)
                dve.wait_ge(v_gate, count + 4)
                nc.vector.tensor_tensor(w_second[:, i], e2[:, i], w_first[:, i], ALU.mult).then_inc(v_gate, 1)
                nc.vector.tensor_tensor(pick1[:, i], pick1[:, i], wide(w_first), ALU.mult).then_inc(v_gate, 1)
                dve.wait_ge(v_gate, count + 5)
                nc.vector.tensor_tensor(pick2[:, i], pick2[:, i], wide(w_second), ALU.mult).then_inc(v_gate, 1)
                dve.wait_ge(v_gate, count + 7)
                nc.vector.tensor_tensor(gate[:, i], pick1[:, i], pick2[:, i], ALU.add).then_inc(v_gate, 2)

            def combine(b, t):
                n = T * b + t
                dve.wait_ge(pe_y, n + 1)
                dve.wait_ge(v_gate, 9 * (b + 1))
                if n >= 2:
                    dve.wait_ge(v_moe, 2 * n - 2)
                nc.vector.tensor_tensor(gated[:, n % 2], slot(F_Y + t)[:, :].rearrange("p (e m) -> p e m", e=E),
                                        gate[:, b % 2, t].unsqueeze(2).to_broadcast([P, E, M]),
                                        ALU.mult).then_inc(v_gated, 1)
                dve.wait_ge(v_gated, n + 1)
                nc.vector.tensor_reduce(moe[:, b % 2, t, 0], gated[:, n % 2].rearrange("p e m -> p m e"), AX_X,
                                        ALU.add).then_inc(v_moe, 1)
                dve.wait_ge(v_moe, 2 * n + 1)
                nc.vector.tensor_copy(moe[:, b % 2, t, 1], moe[:, b % 2, t, 0]).then_inc(v_moe, 1)

            def split_moe(b):
                dve.wait_ge(pe_moeT, b + 1)
                nc.vector.tensor_copy(moe_parts[:, b % 2], slot(F_MT)[:, :]).then_inc(v_mhi, 1)
                dve.wait_ge(v_mhi, b + 1)
                nc.vector.tensor_tensor(moe_parts[M:P, b % 2], slot(F_MT)[M:P, :],
                                        moe_parts[M:P, b % 2].bitcast(F32), ALU.subtract).then_inc(v_mparts, 1)

            def dec_stats(b):
                dve.wait_ge(pe_dec, b + 1)
                statistics(LN_DEC, b, lambda t: slot(F_DEC)[:, t * P:(t + 1) * P])
                for t in range(T):
                    dve.wait_ge(v_mv[LN_DEC], T * b + t + 1)
                    nc.vector.scalar_tensor_tensor(z1[:, b % 2, t], slot(F_DEC)[:, t * P:(t + 1) * P],
                                                   mean(LN_DEC, b, t), g_all[:, :], ALU.subtract,
                                                   ALU.mult).then_inc(v_z1, 1)

            def dec_norm(b):
                dve.wait_ge(g_rstd[LN_DEC], b + 1)
                for t in range(T):
                    dve.wait_ge(v_z1, T * b + t + 1)
                    nc.vector.scalar_tensor_tensor(z[:, b % 2, t], z1[:, b % 2, t], inv(LN_DEC, b, t), b_all[:, :],
                                                   ALU.mult, ALU.add).then_inc(v_z, 1)

            def z_stats(b):
                dve.wait_ge(v_z, T * (b + 1))
                statistics(LN_Z, b, lambda t: z[:, b % 2, t])

            def z_norm(b):
                dve.wait_ge(g_rstd[LN_Z], b + 1)
                for t in range(T):
                    nc.vector.tensor_scalar(zn[:, b % 2, t], z[:, b % 2, t], mean(LN_Z, b, t), inv(LN_Z, b, t),
                                            ALU.subtract, ALU.mult).then_inc(v_zn, 1)
                dve.wait_ge(v_zn, T * (b + 1))
                nc.vector.tensor_tensor(x_out[:, b], zn[:, b % 2], x_mid[:, b], ALU.add).then_inc(v_out, 1)

            x_stats(0)
            dve.wait_ge(pe_bias, 1)
            nc.vector.tensor_copy(bias_cols[:, :], ps_t[:, 0:ROWS]).then_inc(v_bias, 1)
            dve.wait_ge(v_bias, 1)
            nc.vector.tensor_scalar(bq_scaled[:, :], bias_cols[:, R_Q:R_Q + 1], SCALE, None, ALU.mult).then_inc(v_bias2, 1)
            nc.vector.tensor_scalar(bias_half[:, 0:HC], bias_cols[:, R_ENC:R_ENC + HC], 0.5, None,
                                    ALU.mult).then_inc(v_bias2, 1)
            nc.vector.tensor_scalar(bias_half[:, HC:2 * HC], bias_cols[:, R_C2S:R_C2S + HC], 0.5, None,
                                    ALU.mult).then_inc(v_bias2, 1)
            x_norm(0)
            x_stats(1)
            v_out_(0)
            x_norm(1)
            dve.wait_ge(pe_bcont, 1)
            nc.vector.tensor_tensor(b_cont[:, :], ps_o[:, 0:1], bias_cols[:, R_S2C:R_S2C + 1], ALU.add).then_inc(
                v_bcont, 1)
            row_max(0, 0)
            dve.wait_ge(d_w1, 32)
            nc.vector.tensor_copy(w1_hi[:, :, :], w1_raw[:, :, :]).then_inc(v_w1, 1)
            row_max(0, 1)
            dve.wait_ge(v_w1, 1)
            nc.vector.tensor_tensor(w1_lo[:, :, :], w1_raw[:, :, :], w1_hi[:, :, :].bitcast(F32),
                                    ALU.subtract).then_inc(v_w1, 1)
            row_max(0, 2)
            dve.wait_ge(d_c2s, 32)
            nc.vector.tensor_copy(w_c2s_hi[:, :], w_c2s_raw[:, :]).then_inc(v_c2s, 1)
            dve.wait_ge(v_c2s, 1)
            nc.vector.tensor_tensor(w_c2s_lo[:, :], w_c2s_raw[:, :], w_c2s_hi[:, :].bitcast(F32),
                                    ALU.subtract).then_inc(v_c2s, 1)
            row_max(0, 3)

            def split_row(row, rest, hi, mid, stack, s, base):
                nc.vector.tensor_copy(hi, row).then_inc(s, 1)
                dve.wait_ge(s, base + 1)
                nc.vector.tensor_tensor(rest, row, hi, ALU.subtract).then_inc(s, 1)
                dve.wait_ge(s, base + 2)
                nc.vector.tensor_copy(mid, rest).then_inc(s, 1)
                dve.wait_ge(s, base + 3)
                nc.vector.tensor_copy(stack[0:1], hi[0:1]).then_inc(s, 1)
                nc.vector.tensor_copy(stack[32:33], mid[32:33]).then_inc(s, 1)
                nc.vector.tensor_tensor(stack[64:65], rest[64:65], mid[64:65], ALU.subtract).then_inc(s, 1)

            dve.wait_ge(d_b2, 48)
            dve.wait_ge(g_zero_rows, 3)
            split_row(b2_row[:, :], b2_rest[:, :], b2_hi[:, :], b2_mid[:, :], b2_stack[:, :], v_b2, 0)
            v_out_(1)
            attn_stats(0)
            dve.wait_ge(pe_bdec, 1)
            nc.vector.tensor_copy(b_dec_sum[:, :], ps_t[:, 0:D]).then_inc(v_bdec, 2)
            attn_norm(0)
            mid_stats(0)
            dve.wait_ge(v_bdec, 2)
            split_row(b_dec_sum[:, :], b_dec_rest[:, :], b_dec_hi[:, :], b_dec_mid[:, :], b_dec_stack[:, :], v_bdec, 2)
            mid_norm(0)
            dve.wait_ge(v_b2, 6)
            dve.wait_ge(v_bdec, 8)
            dve.wait_ge(d_ln, 32)
            nc.vector.tensor_copy(b2_rest[0:1, 0:1], b2_row[0:1, 0:1]).then_inc(v_b2, 2)
            nc.vector.tensor_copy(b_dec_rest[0:1, 0:1], b2_row[0:1, 0:1]).then_inc(v_bdec, 1)
            for b in range(B):
                n, m = b + 1, b + 2
                more, more2 = n < B, m < B
                if b >= 1:
                    dec_stats(b - 1)
                if more:
                    row_max(n, 0)
                if b >= 1:
                    dec_norm(b - 1)
                if more:
                    row_max(n, 1)
                if b >= 1:
                    z_stats(b - 1)
                split_cont(b)
                if b >= 1:
                    z_norm(b - 1)
                router_top(b)
                if more:
                    row_max(n, 2)
                router_gates(b)
                if more2:
                    x_stats(m)
                if more:
                    row_max(n, 3)
                if more2:
                    x_norm(m)
                combine(b, 0)
                combine(b, 1)
                if more:
                    attn_stats(n)
                combine(b, 2)
                if more:
                    attn_norm(n)
                combine(b, 3)
                if more:
                    mid_stats(n)
                split_moe(b)
                if more2:
                    v_out_(m)
                if more:
                    mid_norm(n)
            dec_stats(B - 1)
            dec_norm(B - 1)
            z_stats(B - 1)
            z_norm(B - 1)


_INS = ["L0_attn_x", "L0_attn_Wq", "L0_attn_bq", "L0_attn_Wk", "L0_attn_bk", "L0_attn_Wv", "L0_attn_bv",
        "L0_ffn_W_enc", "L0_ffn_b_enc", "L0_ffn_W_s2c", "L0_ffn_b_s2c", "L0_ffn_Wr", "L0_ffn_br", "L0_ffn_W1",
        "L0_ffn_b1", "L0_ffn_W2", "L0_ffn_b2", "L0_ffn_W_c2s", "L0_ffn_b_c2s", "L0_ffn_W_dec", "L0_ffn_b_dec",
        "L0_ffn_ln_g", "L0_ffn_ln_b"]


def kernel(**inputs):
    import numpy as _np
    import concourse.bacc as _bacc
    from concourse import mybir as _mybir
    from concourse.bass_utils import run_bass_kernel_spmd as _run

    nc = _bacc.Bacc("TRN2", target_bir_lowering=False, num_devices=1)
    arrays, args = {}, []
    for name in _INS:
        a = _np.ascontiguousarray(inputs[name])
        arrays[f"in_{name}"] = a
        args.append(nc.dram_tensor(f"in_{name}", a.shape, _mybir.dt.from_np(a.dtype), kind="ExternalInput").ap())
    shape = tuple(inputs["L0_attn_x"].shape)
    args.append(nc.dram_tensor("out", shape, _mybir.dt.float32, kind="ExternalOutput").ap())
    attention_moe_block(nc, *args)
    r = _run(nc, [arrays], core_ids=[0])
    return r.results[0]["out"]
```

```python
from contextlib import ExitStack

import concourse.bass as bass
from concourse import mybir

ALU = mybir.AluOpType
ACT = mybir.ActivationFunctionType
AX_X = mybir.AxisListType.X
F32 = mybir.dt.float32
F32R = mybir.dt.float32r
BF16 = mybir.dt.bfloat16
U32 = mybir.dt.uint32

P = 128
EPS = 1e-5


def attention_moe_block(
    nc: bass.Bass,
    x, Wq, bq, Wk, bk, Wv, bv,
    W_enc, b_enc, W_s2c, b_s2c, Wr, br, W1, b1, W2, b2,
    W_c2s, b_c2s, W_dec, b_dec, ln_g, ln_b,
    out,
):
    B, S, D = x.shape
    H = W_enc.shape[1]
    M = W_s2c.shape[1]
    E = Wr.shape[1]
    EH = W1.shape[2]
    T = S // P
    TH = T // 2
    HC = H // P
    assert D == P and EH == P and M == 64 and E == 8 and T * D == 512 and E * M == 512
    SCALE = float(D) ** -0.5

    R_Q, R_K, R_ENC, R_C2S, R_B1 = 0, 1, 2, 2 + HC, 2 + 2 * HC
    R_S2C = R_B1 + E
    ROWS = R_S2C + 1

    x_dram = x.rearrange("b (p t) d -> b p t d", t=T)
    out_dram = out.rearrange("b (p t) d -> b p t d", t=T)

    with ExitStack() as ctx:
        def sb(name, shape, dt=F32):
            return ctx.enter_context(nc.sbuf_tensor(name, shape, dt))

        def psum(name):
            return ctx.enter_context(nc.psum_tensor(name, [P, 512], F32))

        def sem(name):
            return ctx.enter_context(nc.semaphore(name))

        ident = sb("ident", [P, P])
        ones = sb("ones", [P, P])
        ones_bf = sb("ones_bf", [P, P], BF16)
        expert_no = sb("expert_no", [P, E])
        minus_half = sb("minus_half", [P, TH])
        wq = sb("wq", [P, D])
        wk = sb("wk", [P, D])
        wv = sb("wv", [P, D])
        bv_all = sb("bv_all", [P, D])
        bias_rows = sb("bias_rows", [ROWS, P])
        bias_cols = sb("bias_cols", [P, ROWS])
        bias_half = sb("bias_half", [P, 2 * HC])
        bq_scaled = sb("bq_scaled", [P, 1])
        w_enc = sb("w_enc", [P, H])
        w_s2c_raw = sb("w_s2c_raw", [P, HC, M])
        w_s2c = sb("w_s2c", [P, HC, 2, M])
        b_cont = sb("b_cont", [P, 1])
        w_r = sb("w_r", [M, E])
        br_all = sb("br_all", [P, E])
        w1_raw = sb("w1_raw", [P, E, EH])
        w1_hi = sb("w1_hi", [P, E, EH], F32R)
        w1_lo = sb("w1_lo", [P, E, EH], F32R)
        w2 = sb("w2", [P, E, M])
        b2_all = sb("b2_all", [P, E * M])
        b2_rest = sb("b2_rest", [P, E * M])
        b2_hi = sb("b2_hi", [P, E * M], BF16)
        b2_mid = sb("b2_mid", [P, E * M], BF16)
        b2_stack = sb("b2_stack", [P, E * M], BF16)
        w_c2s_raw = sb("w_c2s_raw", [P, H])
        w_c2s_hi = sb("w_c2s_hi", [P, H], F32R)
        w_c2s_lo = sb("w_c2s_lo", [P, H], F32R)
        w_dec_raw = sb("w_dec_raw", [P, HC, D])
        w_dec = sb("w_dec", [P, HC, D])
        b_dec_row = sb("b_dec_row", [1, D])
        b_dec_sum = sb("b_dec_sum", [P, D])
        b_dec_rest = sb("b_dec_rest", [P, D])
        b_dec_hi = sb("b_dec_hi", [P, D], BF16)
        b_dec_mid = sb("b_dec_mid", [P, D], BF16)
        b_dec_stack = sb("b_dec_stack", [P, D], BF16)
        g_all = sb("g_all", [P, D])
        b_all = sb("b_all", [P, D])

        x_in = sb("x_in", [P, B, T, D])
        x_mid = sb("x_mid", [P, B, T, D])
        x_out = sb("x_out", [P, B, T, D])
        xn = sb("xn", [P, 2, T, D])
        xnT = sb("xnT", [P, 2, S])
        qT = sb("qT", [P, 2, S])
        kT = sb("kT", [P, 2, S])
        v = sb("v", [P, 2, T, D])
        neg_max = sb("neg_max", [P, 2, T])
        prob_sum = sb("prob_sum", [P, 2, T])
        probs = sb("probs", [P, 2, T, S])
        probsT = sb("probsT", [P, 2, T, T, P])
        attn = sb("attn", [P, 2, T, D])
        hn = sb("hn", [P, 2, T, D])
        hT = sb("hT", [P, 2, S])
        spikes = sb("spikes", [P, 2, HC, S])
        cont = sb("cont", [P, 2, S])
        cont_parts = sb("cont_parts", [P, 2, S], F32R)
        logits = sb("logits", [P, 2, T, E])
        top = sb("top", [P, 2, T, 8])
        top_no = sb("top_no", [P, 2, T, 8], U32)
        top_diff = sb("top_diff", [P, 2, T])
        e2 = sb("e2", [P, 2, T])
        e_sum = sb("e_sum", [P, 2, T])
        w_first = sb("w_first", [P, 2, T])
        w_second = sb("w_second", [P, 2, T])
        pick1 = sb("pick1", [P, 2, T, E])
        pick2 = sb("pick2", [P, 2, T, E])
        gate = sb("gate", [P, 2, T, E])
        hidden = sb("hidden", [P, E, S])
        gated = sb("gated", [P, 2, E, M])
        moe = sb("moe", [P, 2, T, 2, M])
        moe_parts = sb("moe_parts", [P, 2, S], F32R)
        spikes2 = sb("spikes2", [P, 2, HC, S])
        z1 = sb("z1", [P, 2, T, D])
        z = sb("z", [P, 2, T, D])
        zn = sb("zn", [P, 2, T, D])

        LN_X, LN_ATT, LN_MID, LN_DEC, LN_Z = range(5)
        stats = sb("stats", [P, 5, 2, T, 6])
        mean_var = sb("mean_var", [P, 5, 2, T, 2])
        eps_term = sb("eps_term", [P, 2, T])
        var_eps = sb("var_eps", [P, 5, 2, T])
        rstd = sb("rstd", [P, 5, 2, T])
        warm = sb("warm", [P, 1])

        ps_s = [psum("ps_s0"), psum("ps_s1")]
        ps_t = psum("ps_t")
        ps_a = psum("ps_a")
        ps_o = psum("ps_o")
        ring = [psum("ps_f0"), psum("ps_f1"), psum("ps_f2")]
        F_HT, F_ENC, F_MT, F_C2S, F_CONT, F_DEC, F_LOGIT, F_H = 0, (1, 3), 2, (4, 5), 6, 7, 8, 9
        F_Y = F_H + E
        assert (F_Y + T) % 3 == 0
        def slot(product):
            return ring[product % 3]

        d_x = [sem(f"d_x{b}") for b in range(B)]
        d_qkv = sem("d_qkv")
        d_rows = sem("d_rows")
        d_enc = sem("d_enc")
        d_s2c = sem("d_s2c")
        d_router = sem("d_router")
        d_w1 = sem("d_w1")
        d_w2 = sem("d_w2")
        d_b2 = sem("d_b2")
        d_c2s = sem("d_c2s")
        d_dec = sem("d_dec")
        d_ln = sem("d_ln")
        d_out = sem("d_out")

        g_zero = sem("g_zero")
        g_const = sem("g_const")
        g_s2c = sem("g_s2c")
        g_dec = sem("g_dec")
        g_zero_rows = sem("g_zero_rows")
        g_warm = sem("g_warm")
        v_veps = [sem(f"v_veps{n}") for n in range(5)]
        v_k0 = sem("v_k0")
        a_warm = sem("a_warm")
        g_rstd = [sem(f"g_rstd{n}") for n in range(5)]

        pe_bias = sem("pe_bias")
        pe_bcont = sem("pe_bcont")
        pe_bdec = sem("pe_bdec")
        pe_xnT = sem("pe_xnT")
        pe_q = sem("pe_q")
        pe_k = sem("pe_k")
        pe_v = sem("pe_v")
        pe_s = sem("pe_s")
        pe_pT = sem("pe_pT")
        pe_o = sem("pe_o")
        pe_hT = sem("pe_hT")
        pe_enc = sem("pe_enc")
        pe_cont = sem("pe_cont")
        pe_logit = sem("pe_logit")
        pe_h = sem("pe_h")
        pe_y = sem("pe_y")
        pe_moeT = sem("pe_moeT")
        pe_c2s = sem("pe_c2s")
        pe_dec = sem("pe_dec")

        a_xnT = sem("a_xnT")
        a_q = sem("a_q")
        a_k = sem("a_k")
        a_exp = sem("a_exp")
        a_pT = sem("a_pT")
        a_hT = sem("a_hT")
        a_enc = sem("a_enc")
        a_cont = sem("a_cont")
        a_e2 = sem("a_e2")
        a_h = sem("a_h")
        a_c2s = sem("a_c2s")

        v_bias = sem("v_bias")
        v_bias2 = sem("v_bias2")
        v_bcont = sem("v_bcont")
        v_w1 = sem("v_w1")
        v_c2s = sem("v_c2s")
        v_b2 = sem("v_b2")
        v_bdec = sem("v_bdec")
        v_stats = [sem(f"v_stats{n}") for n in range(5)]
        v_mv = [sem(f"v_mv{n}") for n in range(5)]
        v_xn = sem("v_xn")
        v_v = sem("v_v")
        v_max = sem("v_max")
        v_epst = sem("v_epst")
        v_attn = sem("v_attn")
        v_hn = sem("v_hn")
        v_mid = sem("v_mid")
        v_hi = sem("v_hi")
        v_cont = sem("v_cont")
        v_logit = sem("v_logit")
        v_top = sem("v_top")
        v_topno = sem("v_topno")
        v_diff = sem("v_diff")
        v_gate = sem("v_gate")
        v_gated = sem("v_gated")
        v_moe = sem("v_moe")
        v_moe2 = sem("v_moe2")
        v_mhi = sem("v_mhi")
        v_mparts = sem("v_mparts")
        v_z1 = sem("v_z1")
        v_z = sem("v_z")
        v_zn = sem("v_zn")
        v_out = sem("v_out")

        block = ctx.enter_context(nc.Block())

        @block.sync
        def _(sp):
            def row(vec, n=1):
                return vec.rearrange("(a d) -> a d", a=n)

            sp.dma_start(x_in[:, 0], x_dram[0]).then_inc(d_x[0], 16)
            sp.dma_start(wq[:, :], Wq).then_inc(d_qkv, 16)
            sp.dma_start(bias_rows[R_Q:R_Q + 1, :], row(bq)).then_inc(d_rows, 16)
            sp.dma_start(bias_rows[R_K:R_K + 1, :], row(bk)).then_inc(d_rows, 16)
            sp.dma_start(wk[:, :], Wk).then_inc(d_qkv, 16)
            sp.dma_start(bias_rows[R_ENC:R_ENC + HC, :], row(b_enc, HC)).then_inc(d_rows, 16)
            sp.dma_start(bias_rows[R_C2S:R_C2S + HC, :], row(b_c2s, HC)).then_inc(d_rows, 16)
            sp.dma_start(bias_rows[R_B1:R_B1 + E, :], b1).then_inc(d_rows, 16)
            for half in range(2):
                sp.dma_start(bias_rows[R_S2C:R_S2C + 1, half * M:(half + 1) * M], row(b_s2c)).then_inc(d_rows, 16)
            sp.dma_start(wv[:, :], Wv).then_inc(d_qkv, 16)
            sp.dma_start(bv_all[:, :], bv.partition_broadcast(P)).then_inc(d_qkv, 16)
            sp.dma_start(x_in[:, 1], x_dram[1]).then_inc(d_x[1], 16)
            sp.dma_start(w_s2c_raw[:, :, :], W_s2c.rearrange("(c p) m -> p c m", p=P)).then_inc(d_s2c, 16)
            for half in range(2):
                sp.dma_start(w1_raw[half * M:(half + 1) * M], W1.rearrange("e m h -> m e h")).then_inc(d_w1, 16)
            sp.dma_start(w_enc[:, :], W_enc).then_inc(d_enc, 16)
            sp.dma_start(w_r[:, :], Wr).then_inc(d_router, 16)
            sp.dma_start(br_all[:, :], br.partition_broadcast(P)).then_inc(d_router, 16)
            sp.dma_start(b2_all[:, :], b2.rearrange("e m -> (e m)").partition_broadcast(P)).then_inc(d_b2, 16)
            sp.dma_start(w2[:, :, :], W2.rearrange("e h m -> h e m")).then_inc(d_w2, 16)
            sp.dma_start(w_dec_raw[:, :, :], W_dec.rearrange("(c p) d -> p c d", p=P)).then_inc(d_dec, 16)
            sp.dma_start(b_dec_row[:, :], row(b_dec)).then_inc(d_dec, 16)
            for half in range(2):
                sp.dma_start(w_c2s_raw[half * M:(half + 1) * M], W_c2s).then_inc(d_c2s, 16)
            sp.dma_start(x_in[:, 2], x_dram[2]).then_inc(d_x[2], 16)
            sp.dma_start(g_all[:, :], ln_g.partition_broadcast(P)).then_inc(d_ln, 16)
            sp.dma_start(b_all[:, :], ln_b.partition_broadcast(P)).then_inc(d_ln, 16)
            sp.dma_start(x_in[:, 3], x_dram[3]).then_inc(d_x[3], 16)
            for b in range(B):
                for h in range(2):
                    part = slice(TH * h, TH * (h + 1))
                    sp.wait_ge(v_out, 2 * b + h + 1)
                    sp.dma_start(out_dram[b, :, part], x_out[:, b, part]).then_inc(d_out, 16)
            sp.wait_ge(d_out, 16 * 2 * B)

        @block.gpsimd
        def _(pool):
            nc.gpsimd.memset(ident[:, :], 0.0).then_inc(g_zero, 1)
            nc.gpsimd.memset(warm[:, :], 0.0).then_inc(g_warm, 1)
            nc.gpsimd.memset(minus_half[:, :], -0.5).then_inc(g_const, 1)
            pool.wait_ge(g_zero, 1)
            nc.gpsimd.affine_select(out=ident[:, :], in_=ident[:, :], compare_op=ALU.not_equal, fill=1.0, base=0,
                                    pattern=[[-1, P]], channel_multiplier=1).then_inc(g_const, 1)

            def inverse_std(n, b, h):
                part = (slice(None), n, b % 2, slice(TH * h, TH * (h + 1)))
                pool.wait_ge(v_veps[n], 2 * b + h + 1)
                nc.gpsimd.tensor_tensor(rstd[part], var_eps[part], minus_half[:, :], ALU.pow).then_inc(g_rstd[n], 1)

            pool.wait_ge(g_const, 2)
            for h in range(2):
                inverse_std(LN_X, 0, h)
            nc.gpsimd.memset(ones[:, :], 1.0).then_inc(g_const, 1)
            nc.gpsimd.memset(ones_bf[:, :], 1.0).then_inc(g_const, 1)
            for h in range(2):
                inverse_std(LN_X, 1, h)
            pool.wait_ge(d_s2c, 16)
            for half in range(2):
                nc.gpsimd.tensor_scalar(w_s2c[:, :, half], w_s2c_raw[:, :, :], 0.5, None, ALU.mult).then_inc(g_s2c, 1)
            nc.gpsimd.memset(b_dec_stack[:, :], 0.0).then_inc(g_zero_rows, 1)
            nc.gpsimd.memset(b2_stack[:, :], 0.0).then_inc(g_zero_rows, 1)
            for e in range(E):
                nc.gpsimd.memset(expert_no[:, e:e + 1], float(e)).then_inc(g_const, 1)
            pool.wait_ge(d_dec, 32)
            nc.gpsimd.tensor_scalar(w_dec[:, :, :], w_dec_raw[:, :, :], 0.5, None, ALU.mult).then_inc(g_dec, 1)
            for n in (LN_ATT, LN_MID):
                for h in range(2):
                    inverse_std(n, 0, h)
            for b in range(B + 1):
                for n in (LN_DEC, LN_Z):
                    for h in range(2 if b >= 1 else 0):
                        inverse_std(n, b - 1, h)
                for h in range(2 if b + 2 < B else 0):
                    inverse_std(LN_X, b + 2, h)
                for h in range(2 if b + 1 < B else 0):
                    inverse_std(LN_ATT, b + 1, h)
                    inverse_std(LN_MID, b + 1, h)

        @block.scalar
        def _(act):
            def xnT_out(b):
                act.wait_ge(pe_xnT, b + 1)
                nc.scalar.activation(xnT[:, b % 2], ps_a[:, :], ACT.Identity).then_inc(a_xnT, 1)

            def q_out(b):
                act.wait_ge(pe_q, b + 1)
                nc.scalar.activation(qT[:, b % 2], ps_a[:, :], ACT.Identity, bias=bq_scaled[:, :],
                                     scale=SCALE).then_inc(a_q, 1)

            def k_out(b):
                act.wait_ge(pe_k, b + 1)
                nc.scalar.activation(kT[:, b % 2], ps_a[:, :], ACT.Identity,
                                     bias=bias_cols[:, R_K:R_K + 1]).then_inc(a_k, 1)

            def exps(b, t):
                act.wait_ge(v_max, T * b + t + 1)
                nc.scalar.activation(probs[:, b % 2, t], ps_s[t % 2][:, :], ACT.Exp, bias=neg_max[:, b % 2, t:t + 1],
                                     accum_out=prob_sum[:, b % 2, t:t + 1]).then_inc(a_exp, 1)

            def pT_out(b, t):
                act.wait_ge(pe_pT, T * b + t + 1)
                nc.scalar.activation(probsT[:, b % 2, t], ps_t[:, :].rearrange("p (k q) -> p k q", k=T),
                                     ACT.Identity).then_inc(a_pT, 1)

            def hT_out(b):
                act.wait_ge(pe_hT, b + 1)
                nc.scalar.activation(hT[:, b % 2], slot(F_HT)[:, :], ACT.Identity).then_inc(a_hT, 1)

            def encode(b, c):
                act.wait_ge(pe_enc, HC * b + c + 1)
                nc.scalar.activation(spikes[:, b % 2, c], slot(F_ENC[c])[:, :], ACT.Tanh,
                                     bias=bias_half[:, c:c + 1], scale=0.5).then_inc(a_enc, 1)

            def cont_out(b):
                act.wait_ge(pe_cont, b + 1)
                if b == 0:
                    act.wait_ge(v_bcont, 1)
                nc.scalar.activation(cont[:, b % 2], slot(F_CONT)[:, :], ACT.Identity,
                                     bias=b_cont[:, :]).then_inc(a_cont, 1)

            def second_exp(b):
                act.wait_ge(v_diff, b + 1)
                nc.scalar.activation(e2[:, b % 2], top_diff[:, b % 2], ACT.Exp).then_inc(a_e2, 1)

            def relu(b, e):
                act.wait_ge(pe_h, E * b + e + 1)
                if e == 0 and b >= 1:
                    act.wait_ge(pe_y, T * b)
                nc.scalar.activation(hidden[:, e], slot(F_H + e)[:, :], ACT.Relu,
                                     bias=bias_cols[:, R_B1 + e:R_B1 + e + 1]).then_inc(a_h, 1)

            def spike(b, c):
                act.wait_ge(pe_c2s, HC * b + c + 1)
                nc.scalar.activation(spikes2[:, b % 2, c], slot(F_C2S[c])[:, :], ACT.Tanh,
                                     bias=bias_half[:, HC + c:HC + c + 1], scale=0.5).then_inc(a_c2s, 1)

            act.wait_ge(g_warm, 1)
            nc.scalar.activation(warm[:, :], warm[:, :], ACT.Exp).then_inc(a_warm, 1)
            xnT_out(0)
            act.wait_ge(v_bias2, 3)
            q_out(0)
            xnT_out(1)
            exps(0, 0)
            pT_out(0, 0)
            q_out(1)
            exps(0, 1)
            pT_out(0, 1)
            exps(0, 2)
            k_out(1)
            pT_out(0, 2)
            exps(0, 3)
            pT_out(0, 3)
            exps(1, 0)
            exps(1, 1)
            hT_out(0)
            for c in range(HC):
                encode(0, c)
            cont_out(0)
            for b in range(B):
                n, m = b + 1, b + 2
                more, more2 = n < B, m < B
                relu(b, 0)
                if more:
                    pT_out(n, 0)
                relu(b, 1)
                if more:
                    exps(n, 2)
                relu(b, 2)
                second_exp(b)
                if more:
                    pT_out(n, 1)
                relu(b, 3)
                if more:
                    exps(n, 3)
                relu(b, 4)
                if more:
                    pT_out(n, 2)
                relu(b, 5)
                relu(b, 6)
                if more:
                    pT_out(n, 3)
                relu(b, 7)
                if more2:
                    xnT_out(m)
                    q_out(m)
                    k_out(m)
                if more:
                    hT_out(n)
                    for c in range(HC):
                        encode(n, c)
                if more2:
                    exps(m, 0)
                for c in range(HC):
                    spike(b, c)
                if more:
                    cont_out(n)
                if more2:
                    exps(m, 1)

        @block.tensor
        def _(pe):
            def turn_x(b):
                pe.wait_ge(v_xn, T * (b + 1))
                if b == 0:
                    pe.wait_ge(g_const, 2)
                elif b == 1:
                    pe.wait_ge(a_q, 1)
                else:
                    pe.wait_ge(v_attn, T * (b - 1) + TH)
                for t in range(T):
                    mm = nc.tensor.transpose(ps_a[:, t * P:(t + 1) * P], xn[:, b % 2, t], ident[:, :])
                mm.then_inc(pe_xnT, 1)

            def project_q(b):
                pe.wait_ge(a_xnT, b + 1)
                if b == 0:
                    pe.wait_ge(d_qkv, 64)
                nc.tensor.matmul(ps_a[:, :], wq[:, :], xnT[:, b % 2], start=True, stop=True).then_inc(pe_q, 1)

            def project_k(b):
                if b >= 1:
                    pe.wait_ge(a_q, b + 1)
                nc.tensor.matmul((ps_a if b else ps_s[1])[:, :], wk[:, :], xnT[:, b % 2],
                                 start=True, stop=True).then_inc(pe_k, 1)

            def project_v(b):
                if b >= 1:
                    pe.wait_ge(a_k, b)
                for t in range(T):
                    mm = nc.tensor.matmul((ps_a if b else ps_t)[:, t * P:(t + 1) * P],
                                          xnT[:, b % 2, t * P:(t + 1) * P], wv[:, :], start=True, stop=True)
                mm.then_inc(pe_v, 1)

            def scores(b, t):
                if t == 0 and b == 0:
                    pe.wait_ge(a_q, 1)
                    pe.wait_ge(v_k0, 1)
                elif t == 0:
                    pe.wait_ge(a_k, b)
                if T * b + t >= 2:
                    pe.wait_ge(a_exp, T * b + t - 1)
                nc.tensor.matmul(ps_s[t % 2][:, :], qT[:, b % 2, t * P:(t + 1) * P], kT[:, b % 2],
                                 start=True, stop=True).then_inc(pe_s, 1)

            def turn_probs(b, t):
                pe.wait_ge(a_exp, T * b + t + 1)
                if T * b + t >= 1:
                    pe.wait_ge(a_pT, T * b + t)
                else:
                    pe.wait_ge(v_v, 1)
                for k in range(T):
                    mm = nc.tensor.transpose(ps_t[:, k * P:(k + 1) * P], probs[:, b % 2, t, k * P:(k + 1) * P],
                                             ident[:, :])
                mm.then_inc(pe_pT, 1)

            def attend(b, t):
                pe.wait_ge(a_pT, T * b + t + 1)
                if t == 0:
                    pe.wait_ge(v_v, b + 1)
                if t == 0 and b == 0:
                    pe.wait_ge(a_q, 2)
                if t == TH and b >= 1:
                    pe.wait_ge(v_attn, T * b)
                for k in range(T):
                    mm = nc.tensor.matmul((ps_o if t >= TH or b == 0 else ps_a)[:, t * P:(t + 1) * P], probsT[:, b % 2, t, k], v[:, b % 2, k],
                                          start=(k == 0), stop=(k == T - 1))
                if t % TH == TH - 1:
                    mm.then_inc(pe_o, 1)

            def turn_h(b):
                pe.wait_ge(v_hn, T * (b + 1))
                if b >= 1:
                    pe.wait_ge(v_gated, T * b - 2)
                for t in range(T):
                    mm = nc.tensor.transpose(slot(F_HT)[:, t * P:(t + 1) * P], hn[:, b % 2, t], ident[:, :])
                mm.then_inc(pe_hT, 1)

            def encode(b, c):
                pe.wait_ge(a_hT, b + 1)
                if b == 0:
                    pe.wait_ge(d_enc, 16)
                else:
                    pe.wait_ge(v_gated, T * b - 1)
                nc.tensor.matmul(slot(F_ENC[c])[:, :], w_enc[:, c * P:(c + 1) * P], hT[:, b % 2],
                                 start=True, stop=True).then_inc(pe_enc, 1)

            def to_cont(b):
                pe.wait_ge(a_enc, HC * (b + 1))
                if b == 0:
                    pe.wait_ge(g_s2c, 2)
                for c in range(HC):
                    mm = nc.tensor.matmul(slot(F_CONT)[:, :], w_s2c[:, c], spikes[:, b % 2, c],
                                          start=(c == 0), stop=(c == HC - 1))
                mm.then_inc(pe_cont, 1)

            def route(b):
                pe.wait_ge(a_cont, b + 1)
                if b == 0:
                    pe.wait_ge(d_router, 32)
                else:
                    pe.wait_ge(a_c2s, HC * b)
                for t in range(T):
                    mm = nc.tensor.matmul(slot(F_LOGIT)[:, t * E:(t + 1) * E], cont[0:M, b % 2, t * P:(t + 1) * P],
                                          w_r[:, :], start=True, stop=True)
                mm.then_inc(pe_logit, 1)

            def hidden_units(b, e):
                if e == 0:
                    pe.wait_ge(v_cont, b + 1)
                    if b == 0:
                        pe.wait_ge(v_w1, 2)
                if e == 1 and b >= 1:
                    pe.wait_ge(v_z1, T * b)
                if e == 2:
                    pe.wait_ge(v_logit, b + 1)
                if e >= 3:
                    pe.wait_ge(a_h, E * b + e - 2)
                nc.tensor.matmul(slot(F_H + e)[:, :], w1_hi[:, e], cont_parts[:, b % 2], start=True, stop=False)
                nc.tensor.matmul(slot(F_H + e)[:, :], w1_lo[:, e], cont_parts[:, b % 2], start=False,
                                 stop=True).then_inc(pe_h, 1)

            def expert_out(b, t):
                if t == 0:
                    if b == 0:
                        pe.wait_ge(d_w2, 16)
                        pe.wait_ge(v_b2, 6)
                if t == T - 1:
                    pe.wait_ge(v_gated, T * b + 1)
                if t < T - 1:
                    pe.wait_ge(a_h, E * b + E - 2 + t)
                y = slot(F_Y + t)
                nc.tensor.matmul(y[:, :], ones_bf[:, :], b2_stack[:, :], start=True, stop=False)
                for e in range(E):
                    if t == 0:
                        pe.wait_ge(a_h, E * b + e + 1)
                    mm = nc.tensor.matmul(y[:, e * M:(e + 1) * M], hidden[:, e, t * P:(t + 1) * P], w2[:, e],
                                          start=False, stop=(e == E - 1))
                mm.then_inc(pe_y, 1)

            def turn_moe(b):
                pe.wait_ge(v_moe2, T * (b + 1))
                for t in range(T):
                    mm = nc.tensor.transpose(slot(F_MT)[:, t * P:(t + 1) * P],
                                             moe[:, b % 2, t].rearrange("p a m -> p (a m)"), ident[:, :])
                mm.then_inc(pe_moeT, 1)

            def to_spikes(b, c):
                pe.wait_ge(v_mparts, b + 1)
                if b + 1 < B:
                    pe.wait_ge(a_enc, HC * (b + 1) + 1)
                if b == 0:
                    pe.wait_ge(v_c2s, 2)
                nc.tensor.matmul(slot(F_C2S[c])[:, :], w_c2s_hi[:, c * P:(c + 1) * P], moe_parts[:, b % 2],
                                 start=True, stop=False)
                nc.tensor.matmul(slot(F_C2S[c])[:, :], w_c2s_lo[:, c * P:(c + 1) * P], moe_parts[:, b % 2],
                                 start=False, stop=True).then_inc(pe_c2s, 1)

            def decode(b):
                pe.wait_ge(a_c2s, HC * (b + 1))
                if b == 0:
                    pe.wait_ge(v_bdec, 8)
                for t in range(T):
                    d = slot(F_DEC)[:, t * P:(t + 1) * P]
                    nc.tensor.matmul(d, ones_bf[:, :], b_dec_stack[:, :], start=True, stop=False)
                    for c in range(HC):
                        mm = nc.tensor.matmul(d, spikes2[:, b % 2, c, t * P:(t + 1) * P], w_dec[:, c],
                                              start=False, stop=(c == HC - 1))
                mm.then_inc(pe_dec, 1)

            turn_x(0)
            pe.wait_ge(d_rows, 16 * 7)
            nc.tensor.transpose(ps_o[:, 0:ROWS], bias_rows[:, :], ident[0:ROWS, 0:ROWS]).then_inc(pe_bias, 1)
            project_q(0)
            project_k(0)
            project_v(0)
            turn_x(1)
            scores(0, 0)
            scores(0, 1)
            project_q(1)
            turn_probs(0, 0)
            pe.wait_ge(g_s2c, 2)
            pe.wait_ge(g_const, 4)
            pe.wait_ge(v_bias, 1)
            for c in range(HC):
                mm = nc.tensor.matmul(ps_o[:, 0:1], w_s2c[:, c], ones[:, 0:1], start=(c == 0), stop=(c == HC - 1))
            mm.then_inc(pe_bcont, 1)
            scores(0, 2)
            pe.wait_ge(v_bcont, 1)
            attend(0, 0)
            turn_probs(0, 1)
            scores(0, 3)
            project_k(1)
            attend(0, 1)
            turn_probs(0, 2)
            project_v(1)
            attend(0, 2)
            turn_probs(0, 3)
            attend(0, 3)
            scores(1, 0)
            scores(1, 1)
            pe.wait_ge(g_dec, 1)
            pe.wait_ge(a_pT, T)
            for c in range(HC):
                nc.tensor.matmul(ps_t[:, 0:D], ones[:, :], w_dec[:, c], start=(c == 0), stop=False)
            nc.tensor.matmul(ps_t[:, 0:D], ones[0:1, :], b_dec_row[:, :], start=False, stop=True).then_inc(pe_bdec, 1)
            turn_h(0)
            for c in range(HC):
                encode(0, c)
            to_cont(0)
            route(0)
            pe.wait_ge(v_bdec, 2)
            for b in range(B):
                n, m = b + 1, b + 2
                more, more2 = n < B, m < B
                hidden_units(b, 0)
                if more:
                    turn_probs(n, 0)
                hidden_units(b, 1)
                if more:
                    scores(n, 2)
                hidden_units(b, 2)
                if more:
                    attend(n, 0)
                    turn_probs(n, 1)
                hidden_units(b, 3)
                if more:
                    scores(n, 3)
                hidden_units(b, 4)
                if more:
                    attend(n, 1)
                    turn_probs(n, 2)
                hidden_units(b, 5)
                hidden_units(b, 6)
                if more:
                    attend(n, 2)
                    turn_probs(n, 3)
                hidden_units(b, 7)
                expert_out(b, 0)
                if more:
                    attend(n, 3)
                expert_out(b, 1)
                if more2:
                    turn_x(m)
                expert_out(b, 2)
                if more2:
                    project_q(m)
                expert_out(b, 3)
                if more2:
                    project_k(m)
                if more:
                    turn_h(n)
                if more2:
                    project_v(m)
                if more:
                    encode(n, 0)
                turn_moe(b)
                if more:
                    encode(n, 1)
                if more2:
                    scores(m, 0)
                for c in range(HC):
                    to_spikes(b, c)
                if more:
                    to_cont(n)
                decode(b)
                if more:
                    route(n)
                if more2:
                    scores(m, 1)

        @block.vector
        def _(dve):
            def statistics(n, b, h, source):
                tiles = range(TH * h, TH * (h + 1))
                part = slice(TH * h, TH * (h + 1))
                for t in tiles:
                    nc.vector.bn_stats(stats[:, n, b % 2, t], source(t)).then_inc(v_stats[n], 1)
                for t in tiles:
                    dve.wait_ge(v_stats[n], T * b + t + 1)
                    nc.vector.bn_aggr(mean_var[:, n, b % 2, t], stats[:, n, b % 2, t]).then_inc(v_mv[n], 1)
                dve.wait_ge(v_mv[n], T * b + TH * (h + 1))
                if n == LN_ATT:
                    nc.vector.tensor_tensor(var_eps[:, n, b % 2, part], mean_var[:, n, b % 2, part, 1],
                                            eps_term[:, b % 2, part], ALU.add).then_inc(v_veps[n], 1)
                else:
                    nc.vector.tensor_scalar(var_eps[:, n, b % 2, part], mean_var[:, n, b % 2, part, 1], EPS, None,
                                            ALU.add).then_inc(v_veps[n], 1)

            def normed(n, b, h, source, result, done):
                dve.wait_ge(g_rstd[n], 2 * b + h + 1)
                for t in range(TH * h, TH * (h + 1)):
                    nc.vector.tensor_scalar(result(t), source(t), mean(n, b, t), inv(n, b, t), ALU.subtract,
                                            ALU.mult).then_inc(done, 1)

            def mean(n, b, t):
                return mean_var[:, n, b % 2, t, 0:1]

            def inv(n, b, t):
                return rstd[:, n, b % 2, t:t + 1]

            def x_stats(b):
                dve.wait_ge(d_x[b], 16)
                for h in range(2):
                    statistics(LN_X, b, h, lambda t: x_in[:, b, t])

            def x_norm(b):
                for h in range(2):
                    normed(LN_X, b, h, lambda t: x_in[:, b, t], lambda t: xn[:, b % 2, t], v_xn)

            def add_bv(b):
                dve.wait_ge(pe_v, b + 1)
                nc.vector.tensor_tensor(v[:, b % 2], (ps_a if b else ps_t)[:, :].rearrange("p (t d) -> p t d", t=T),
                                        bv_all[:, :].unsqueeze(1).to_broadcast([P, T, D]), ALU.add).then_inc(v_v, 1)

            def row_max(b, t):
                dve.wait_ge(pe_s, T * b + t + 1)
                nc.vector.tensor_reduce(neg_max[:, b % 2, t:t + 1], ps_s[t % 2][:, :], AX_X, ALU.max,
                                        negate=True).then_inc(v_max, 1)

            def attn_out(b, t):
                return (ps_o if t >= TH or b == 0 else ps_a)[:, t * P:(t + 1) * P]

            def attn_stats(b, h):
                dve.wait_ge(a_exp, T * b + TH * (h + 1))
                part = slice(TH * h, TH * (h + 1))
                nc.vector.scalar_tensor_tensor(eps_term[:, b % 2, part], prob_sum[:, b % 2, part], EPS,
                                               prob_sum[:, b % 2, part], ALU.mult, ALU.mult).then_inc(v_epst, 1)
                dve.wait_ge(v_epst, 2 * b + h + 1)
                dve.wait_ge(pe_o, 2 if b == 0 else 2 * b + h + 1)
                statistics(LN_ATT, b, h, lambda t: attn_out(b, t))

            def mid_stats(b, h):
                normed(LN_ATT, b, h, lambda t: attn_out(b, t), lambda t: attn[:, b % 2, t], v_attn)
                dve.wait_ge(v_attn, T * b + TH * (h + 1))
                part = slice(TH * h, TH * (h + 1))
                nc.vector.tensor_tensor(x_mid[:, b, part], attn[:, b % 2, part], x_in[:, b, part],
                                        ALU.add).then_inc(v_mid, 1)
                dve.wait_ge(v_mid, 2 * b + h + 1)
                statistics(LN_MID, b, h, lambda t: x_mid[:, b, t])

            def mid_norm(b, h):
                normed(LN_MID, b, h, lambda t: x_mid[:, b, t], lambda t: hn[:, b % 2, t], v_hn)

            def split_cont(b):
                dve.wait_ge(a_cont, b + 1)
                nc.vector.tensor_copy(cont_parts[:, b % 2], cont[:, b % 2]).then_inc(v_hi, 1)
                dve.wait_ge(v_hi, b + 1)
                nc.vector.tensor_tensor(cont_parts[M:P, b % 2], cont[M:P, b % 2],
                                        cont_parts[M:P, b % 2].bitcast(F32), ALU.subtract).then_inc(v_cont, 1)

            def router_top(b):
                i = b % 2
                dve.wait_ge(pe_logit, b + 1)
                nc.vector.tensor_tensor(logits[:, i], slot(F_LOGIT)[:, 0:T * E].rearrange("p (t e) -> p t e", t=T),
                                        br_all[:, :].unsqueeze(1).to_broadcast([P, T, E]), ALU.add).then_inc(v_logit, 1)
                dve.wait_ge(v_logit, b + 1)
                for t in range(T):
                    nc.vector.max(top[:, i, t], logits[:, i, t]).then_inc(v_top, 1)
                for t in range(T):
                    dve.wait_ge(v_top, T * b + t + 1)
                    nc.vector.max_index(top_no[:, i, t], top[:, i, t], logits[:, i, t]).then_inc(v_topno, 1)
                nc.vector.tensor_tensor(top_diff[:, i], top[:, i, :, 1], top[:, i, :, 0], ALU.subtract).then_inc(v_diff, 1)

            def router_gates(b):
                i = b % 2

                def wide(w):
                    return w[:, i].unsqueeze(2).to_broadcast([P, T, E])

                count = 9 * b
                dve.wait_ge(v_topno, T * (b + 1))
                for pick, j in ((pick1, 0), (pick2, 1)):
                    nc.vector.tensor_tensor(pick[:, i], expert_no[:, :].unsqueeze(1).to_broadcast([P, T, E]),
                                            top_no[:, i, :, j:j + 1].to_broadcast([P, T, E]),
                                            ALU.is_equal).then_inc(v_gate, 1)
                dve.wait_ge(a_e2, b + 1)
                nc.vector.tensor_scalar(e_sum[:, i], e2[:, i], 1.0, None, ALU.add).then_inc(v_gate, 1)
                dve.wait_ge(v_gate, count + 3)
                nc.vector.reciprocal(w_first[:, i], e_sum[:, i]).then_inc(v_gate, 1)
                dve.wait_ge(v_gate, count + 4)
                nc.vector.tensor_tensor(w_second[:, i], e2[:, i], w_first[:, i], ALU.mult).then_inc(v_gate, 1)
                nc.vector.tensor_tensor(pick1[:, i], pick1[:, i], wide(w_first), ALU.mult).then_inc(v_gate, 1)
                dve.wait_ge(v_gate, count + 5)
                nc.vector.tensor_tensor(pick2[:, i], pick2[:, i], wide(w_second), ALU.mult).then_inc(v_gate, 1)
                dve.wait_ge(v_gate, count + 7)
                nc.vector.tensor_tensor(gate[:, i], pick1[:, i], pick2[:, i], ALU.add).then_inc(v_gate, 2)

            def double(b, t):
                dve.wait_ge(v_moe, T * b + t + 1)
                nc.vector.tensor_copy(moe[:, b % 2, t, 1], moe[:, b % 2, t, 0]).then_inc(v_moe2, 1)

            def combine(b, t):
                n = T * b + t
                dve.wait_ge(pe_y, n + 1)
                dve.wait_ge(v_gate, 9 * (b + 1))
                if n >= 2:
                    dve.wait_ge(v_moe, n - 1)
                nc.vector.tensor_tensor(gated[:, n % 2], slot(F_Y + t)[:, :].rearrange("p (e m) -> p e m", e=E),
                                        gate[:, b % 2, t].unsqueeze(2).to_broadcast([P, E, M]),
                                        ALU.mult).then_inc(v_gated, 1)
                if t >= 1:
                    double(b, t - 1)
                dve.wait_ge(v_gated, n + 1)
                nc.vector.tensor_reduce(moe[:, b % 2, t, 0], gated[:, n % 2].rearrange("p e m -> p m e"), AX_X,
                                        ALU.add).then_inc(v_moe, 1)
                if t == T - 1:
                    double(b, t)

            def split_moe(b):
                dve.wait_ge(pe_moeT, b + 1)
                nc.vector.tensor_copy(moe_parts[:, b % 2], slot(F_MT)[:, :]).then_inc(v_mhi, 1)
                dve.wait_ge(v_mhi, b + 1)
                nc.vector.tensor_tensor(moe_parts[M:P, b % 2], slot(F_MT)[M:P, :],
                                        moe_parts[M:P, b % 2].bitcast(F32), ALU.subtract).then_inc(v_mparts, 1)

            def dec_stats(b):
                dve.wait_ge(pe_dec, b + 1)
                for h in range(2):
                    statistics(LN_DEC, b, h, lambda t: slot(F_DEC)[:, t * P:(t + 1) * P])
                for t in range(T):
                    nc.vector.scalar_tensor_tensor(z1[:, b % 2, t], slot(F_DEC)[:, t * P:(t + 1) * P],
                                                   mean(LN_DEC, b, t), g_all[:, :], ALU.subtract,
                                                   ALU.mult).then_inc(v_z1, 1)

            def z_stats(b, h):
                dve.wait_ge(g_rstd[LN_DEC], 2 * b + h + 1)
                for t in range(TH * h, TH * (h + 1)):
                    dve.wait_ge(v_z1, T * b + t + 1)
                    nc.vector.scalar_tensor_tensor(z[:, b % 2, t], z1[:, b % 2, t], inv(LN_DEC, b, t), b_all[:, :],
                                                   ALU.mult, ALU.add).then_inc(v_z, 1)
                dve.wait_ge(v_z, T * b + TH * (h + 1))
                statistics(LN_Z, b, h, lambda t: z[:, b % 2, t])

            def z_norm(b, h):
                normed(LN_Z, b, h, lambda t: z[:, b % 2, t], lambda t: zn[:, b % 2, t], v_zn)
                dve.wait_ge(v_zn, T * b + TH * (h + 1))
                part = slice(TH * h, TH * (h + 1))
                nc.vector.tensor_tensor(x_out[:, b, part], zn[:, b % 2, part], x_mid[:, b, part],
                                        ALU.add).then_inc(v_out, 1)

            x_stats(0)
            x_norm(0)
            dve.wait_ge(pe_bias, 1)
            nc.vector.tensor_copy(bias_cols[:, :], ps_o[:, 0:ROWS]).then_inc(v_bias, 1)
            dve.wait_ge(v_bias, 1)
            nc.vector.tensor_scalar(bq_scaled[:, :], bias_cols[:, R_Q:R_Q + 1], SCALE, None, ALU.mult).then_inc(v_bias2, 1)
            nc.vector.tensor_scalar(bias_half[:, 0:HC], bias_cols[:, R_ENC:R_ENC + HC], 0.5, None,
                                    ALU.mult).then_inc(v_bias2, 1)
            nc.vector.tensor_scalar(bias_half[:, HC:2 * HC], bias_cols[:, R_C2S:R_C2S + HC], 0.5, None,
                                    ALU.mult).then_inc(v_bias2, 1)
            x_stats(1)
            x_norm(1)
            dve.wait_ge(pe_k, 1)
            nc.vector.tensor_scalar(kT[:, 0], ps_s[1][:, :], bias_cols[:, R_K:R_K + 1], None, ALU.add).then_inc(v_k0, 1)
            add_bv(0)
            row_max(0, 0)
            row_max(0, 1)
            dve.wait_ge(pe_bcont, 1)
            nc.vector.tensor_tensor(b_cont[:, :], ps_o[:, 0:1], bias_cols[:, R_S2C:R_S2C + 1], ALU.add).then_inc(
                v_bcont, 1)
            row_max(0, 2)
            dve.wait_ge(d_w1, 32)
            nc.vector.tensor_copy(w1_hi[:, :, :], w1_raw[:, :, :]).then_inc(v_w1, 1)
            row_max(0, 3)
            dve.wait_ge(v_w1, 1)
            nc.vector.tensor_tensor(w1_lo[:, :, :], w1_raw[:, :, :], w1_hi[:, :, :].bitcast(F32),
                                    ALU.subtract).then_inc(v_w1, 1)
            add_bv(1)
            attn_stats(0, 0)
            attn_stats(0, 1)
            row_max(1, 0)
            mid_stats(0, 0)
            mid_stats(0, 1)
            row_max(1, 1)
            mid_norm(0, 0)
            mid_norm(0, 1)

            def split_row(row, rest, hi, mid, stack, s, base):
                nc.vector.tensor_copy(hi, row).then_inc(s, 1)
                dve.wait_ge(s, base + 1)
                nc.vector.tensor_tensor(rest, row, hi, ALU.subtract).then_inc(s, 1)
                dve.wait_ge(s, base + 2)
                nc.vector.tensor_copy(mid, rest).then_inc(s, 1)
                dve.wait_ge(s, base + 3)
                nc.vector.tensor_copy(stack[0:1], hi[0:1]).then_inc(s, 1)
                nc.vector.tensor_copy(stack[32:33], mid[32:33]).then_inc(s, 1)
                nc.vector.tensor_tensor(stack[64:65], rest[64:65], mid[64:65], ALU.subtract).then_inc(s, 1)

            dve.wait_ge(pe_bdec, 1)
            nc.vector.tensor_copy(b_dec_sum[:, :], ps_t[:, 0:D]).then_inc(v_bdec, 2)
            dve.wait_ge(d_b2, 16)
            dve.wait_ge(g_zero_rows, 2)
            split_row(b2_all[:, :], b2_rest[:, :], b2_hi[:, :], b2_mid[:, :], b2_stack[:, :], v_b2, 0)
            dve.wait_ge(v_bdec, 2)
            split_row(b_dec_sum[:, :], b_dec_rest[:, :], b_dec_hi[:, :], b_dec_mid[:, :], b_dec_stack[:, :], v_bdec, 2)
            split_cont(0)
            for b in range(B):
                n, m = b + 1, b + 2
                more, more2 = n < B, m < B
                if b == 1:
                    dve.wait_ge(d_ln, 32)
                if b >= 1:
                    dec_stats(b - 1)
                router_top(b)
                if b >= 1 and more:
                    row_max(n, 1)
                if b == 0:
                    dve.wait_ge(d_c2s, 32)
                    dve.wait_ge(g_const, 12)
                    nc.vector.tensor_copy(w_c2s_hi[:, :], w_c2s_raw[:, :]).then_inc(v_c2s, 1)
                    dve.wait_ge(v_c2s, 1)
                    nc.vector.tensor_tensor(w_c2s_lo[:, :], w_c2s_raw[:, :], w_c2s_hi[:, :].bitcast(F32),
                                            ALU.subtract).then_inc(v_c2s, 1)
                for h in range(2 if b >= 1 else 0):
                    z_stats(b - 1, h)
                if more:
                    row_max(n, 2)
                for h in range(2 if b >= 1 else 0):
                    z_norm(b - 1, h)
                router_gates(b)
                if more:
                    row_max(n, 3)
                if more2:
                    x_stats(m)
                if more:
                    attn_stats(n, 0)
                if more2:
                    x_norm(m)
                if more:
                    mid_stats(n, 0)
                combine(b, 0)
                if more:
                    attn_stats(n, 1)
                    mid_norm(n, 0)
                combine(b, 1)
                if more:
                    mid_stats(n, 1)
                combine(b, 2)
                if more:
                    mid_norm(n, 1)
                combine(b, 3)
                if more2:
                    add_bv(m)
                split_moe(b)
                if more2:
                    row_max(m, 0)
                if more:
                    split_cont(n)
            dec_stats(B - 1)
            for h in range(2):
                z_stats(B - 1, h)
            for h in range(2):
                z_norm(B - 1, h)


_INS = ["L0_attn_x", "L0_attn_Wq", "L0_attn_bq", "L0_attn_Wk", "L0_attn_bk", "L0_attn_Wv", "L0_attn_bv",
        "L0_ffn_W_enc", "L0_ffn_b_enc", "L0_ffn_W_s2c", "L0_ffn_b_s2c", "L0_ffn_Wr", "L0_ffn_br", "L0_ffn_W1",
        "L0_ffn_b1", "L0_ffn_W2", "L0_ffn_b2", "L0_ffn_W_c2s", "L0_ffn_b_c2s", "L0_ffn_W_dec", "L0_ffn_b_dec",
        "L0_ffn_ln_g", "L0_ffn_ln_b"]


def kernel(**inputs):
    import numpy as _np
    import concourse.bacc as _bacc
    from concourse import mybir as _mybir
    from concourse.bass_utils import run_bass_kernel_spmd as _run

    nc = _bacc.Bacc("TRN2", target_bir_lowering=False, num_devices=1)
    arrays, args = {}, []
    for name in _INS:
        a = _np.ascontiguousarray(inputs[name])
        arrays[f"in_{name}"] = a
        args.append(nc.dram_tensor(f"in_{name}", a.shape, _mybir.dt.from_np(a.dtype), kind="ExternalInput").ap())
    shape = tuple(inputs["L0_attn_x"].shape)
    args.append(nc.dram_tensor("out", shape, _mybir.dt.float32, kind="ExternalOutput").ap())
    attention_moe_block(nc, *args)
    r = _run(nc, [arrays], core_ids=[0])
    return r.results[0]["out"]
```

```python
from contextlib import ExitStack

import concourse.bass as bass
from concourse import mybir

ALU = mybir.AluOpType
ACT = mybir.ActivationFunctionType
AX_X = mybir.AxisListType.X
F32 = mybir.dt.float32
F32R = mybir.dt.float32r
BF16 = mybir.dt.bfloat16
U32 = mybir.dt.uint32

P = 128
EPS = 1e-5
WARM_UP = 13


def attention_moe_block(
    nc: bass.Bass,
    x, Wq, bq, Wk, bk, Wv, bv,
    W_enc, b_enc, W_s2c, b_s2c, Wr, br, W1, b1, W2, b2,
    W_c2s, b_c2s, W_dec, b_dec, ln_g, ln_b,
    out,
):
    B, S, D = x.shape
    H = W_enc.shape[1]
    M = W_s2c.shape[1]
    E = Wr.shape[1]
    EH = W1.shape[2]
    T = S // P
    TH = T // 2
    HC = H // P
    assert D == P and EH == P and M == 64 and E == 8 and T * D == 512 and E * M == 512
    SCALE = float(D) ** -0.5

    R_Q, R_K, R_ENC, R_C2S, R_B1 = 0, 1, 2, 2 + HC, 2 + 2 * HC
    R_S2C = R_B1 + E
    ROWS = R_S2C + 1

    x_dram = x.rearrange("b (p t) d -> b p t d", t=T)
    out_dram = out.rearrange("b (p t) d -> b p t d", t=T)

    with ExitStack() as ctx:
        def sb(name, shape, dt=F32):
            return ctx.enter_context(nc.sbuf_tensor(name, shape, dt))

        def psum(name):
            return ctx.enter_context(nc.psum_tensor(name, [P, 512], F32))

        def sem(name):
            return ctx.enter_context(nc.semaphore(name))

        ident = sb("ident", [P, P])
        ones = sb("ones", [P, P])
        ones_bf = sb("ones_bf", [P, P], BF16)
        expert_no = sb("expert_no", [P, E])
        minus_half = sb("minus_half", [P, T])
        wq = sb("wq", [P, D])
        wk = sb("wk", [P, D])
        wv = sb("wv", [P, D])
        bv_all = sb("bv_all", [P, D])
        bias_rows = sb("bias_rows", [ROWS, P])
        bias_cols = sb("bias_cols", [P, ROWS])
        bias_half = sb("bias_half", [P, 2 * HC])
        bq_scaled = sb("bq_scaled", [P, 1])
        w_enc = sb("w_enc", [P, H])
        w_s2c_raw = sb("w_s2c_raw", [P, HC, M])
        w_s2c = sb("w_s2c", [P, HC, 2, M])
        b_cont = sb("b_cont", [P, 1])
        w_r_raw = sb("w_r_raw", [P, E])
        w_r = sb("w_r", [P, 2, E], F32R)
        br_all = sb("br_all", [P, E])
        w1_raw = sb("w1_raw", [P, E, EH])
        w1_hi = sb("w1_hi", [P, E, EH], F32R)
        w1_lo = sb("w1_lo", [P, E, EH], F32R)
        w2 = sb("w2", [P, E, M])
        b2_all = sb("b2_all", [P, E * M])
        b2_rest = sb("b2_rest", [P, E * M])
        b2_hi = sb("b2_hi", [P, E * M], BF16)
        b2_mid = sb("b2_mid", [P, E * M], BF16)
        b2_stack = sb("b2_stack", [P, E * M], BF16)
        w_c2s_raw = sb("w_c2s_raw", [P, H])
        w_c2s_hi = sb("w_c2s_hi", [P, H], F32R)
        w_c2s_lo = sb("w_c2s_lo", [P, H], F32R)
        w_dec_raw = sb("w_dec_raw", [P, HC, D])
        w_dec = sb("w_dec", [P, HC, D])
        b_dec_row = sb("b_dec_row", [1, D])
        b_dec_sum = sb("b_dec_sum", [P, D])
        b_dec_rest = sb("b_dec_rest", [P, D])
        b_dec_hi = sb("b_dec_hi", [P, D], BF16)
        b_dec_mid = sb("b_dec_mid", [P, D], BF16)
        b_dec_stack = sb("b_dec_stack", [P, D], BF16)
        g_all = sb("g_all", [P, D])
        b_all = sb("b_all", [P, D])

        x_in = sb("x_in", [P, B, T, D])
        x_mid = sb("x_mid", [P, B, T, D])
        x_out = sb("x_out", [P, B, T, D])
        xn = sb("xn", [P, 2, T, D])
        xnT = sb("xnT", [P, 2, S])
        qT = sb("qT", [P, 2, S])
        kT = sb("kT", [P, 2, S])
        v = sb("v", [P, 2, T, D])
        neg_max = sb("neg_max", [P, 2, T])
        prob_sum = sb("prob_sum", [P, 2, T])
        probs = sb("probs", [P, 2, T, S])
        probsT = sb("probsT", [P, 2, T, T, P])
        attn = sb("attn", [P, 2, T, D])
        hn = sb("hn", [P, 2, T, D])
        hT = sb("hT", [P, 2, S])
        spikes = sb("spikes", [P, 2, HC, S])
        cont_parts = sb("cont_parts", [P, 2, S], F32R)
        products = sb("products", [P, 2, T, E])
        logits = sb("logits", [P, 2, T, E])
        top = sb("top", [P, 2, T, 8])
        top_no = sb("top_no", [P, 2, T, 8], U32)
        top_diff = sb("top_diff", [P, 2, T])
        e2 = sb("e2", [P, 2, T])
        e_sum = sb("e_sum", [P, 2, T])
        w_first = sb("w_first", [P, 2, T])
        w_second = sb("w_second", [P, 2, T])
        pick1 = sb("pick1", [P, 2, T, E])
        pick2 = sb("pick2", [P, 2, T, E])
        gate = sb("gate", [P, 2, T, E])
        hidden = sb("hidden", [P, E, S])
        gated = sb("gated", [P, 2, E, M])
        moe = sb("moe", [P, 2, T, 2, M])
        moe_parts = sb("moe_parts", [P, 2, S], F32R)
        spikes2 = sb("spikes2", [P, 2, HC, S])
        z1 = sb("z1", [P, 2, T, D])
        z = sb("z", [P, 2, T, D])
        zn = sb("zn", [P, 2, T, D])

        LN_X, LN_ATT, LN_MID, LN_DEC, LN_Z = range(5)

        LAST = [(0, TH), (TH, T)]

        def parts(n, b):
            if n in (LN_DEC, LN_Z) and b == B - 1:
                return LAST
            return [(0, TH), (TH, T)] if n in (LN_ATT, LN_MID) or b < 2 and n == LN_X else [(0, T)]

        def parts_done(n, b, i):
            return sum(len(parts(n, k)) for k in range(b)) + i + 1

        stats = sb("stats", [P, 5, 2, T, 6])
        mean_var = sb("mean_var", [P, 5, 2, T, 2])
        eps_term = sb("eps_term", [P, 2, T])
        var_eps = sb("var_eps", [P, 5, 2, T])
        rstd = sb("rstd", [P, 5, 2, T])
        warm = sb("warm", [P, 1])
        zeros = sb("zeros", [P, 4 * P], BF16)

        ps_s = [psum("ps_s0"), psum("ps_s1")]
        ps_t = psum("ps_t")
        ps_a = psum("ps_a")
        ps_o = psum("ps_o")
        ring = [psum("ps_f0"), psum("ps_f1"), psum("ps_f2")]
        F_HT, F_ENC, F_MT, F_C2S, F_CONT, F_DEC, F_LOGIT, F_H = 0, (1, 3), 2, (4, 5), 6, 7, 8, 9
        F_Y = F_H + E
        assert (F_Y + T) % 3 == 0
        def slot(product):
            return ring[product % 3]

        def hidden_bank(b, e):
            apart = {1: ps_t, 2: ps_s[0], 4: ps_s[1], 7: ps_t} if b == B - 1 else {}
            return apart.get(e, slot(F_H + e))

        def turned_bank(b):
            return ps_s[0] if b == B - 1 else slot(F_HT)

        def encode_bank(b, c):
            return (ps_s[1], ps_t)[c] if b == B - 1 else slot(F_ENC[c])

        def logit_bank(b):
            return ps_o if b == B - 1 else slot(F_LOGIT)

        def attn_out(b, t):
            first_half = ring[2] if b == 0 else ps_a
            return (ps_o if t >= TH else first_half)[:, t * P:(t + 1) * P]

        last_moeT = [ps_s[0], ps_o]
        last_c2s = [[ps_s[1], ps_t], [slot(F_Y + 1), slot(F_Y + 2)]]
        last_dec = [ps_a, slot(F_Y + 3)]

        d_x = [sem(f"d_x{b}") for b in range(B)]
        d_qkv = sem("d_qkv")
        d_rows = sem("d_rows")
        d_enc = sem("d_enc")
        d_s2c = sem("d_s2c")
        d_router = sem("d_router")
        d_w1 = sem("d_w1")
        d_w2 = sem("d_w2")
        d_b2 = sem("d_b2")
        d_c2s = sem("d_c2s")
        d_dec = sem("d_dec")
        d_ln = sem("d_ln")
        d_out = sem("d_out")

        g_zero = sem("g_zero")
        g_const = sem("g_const")
        g_s2c = sem("g_s2c")
        g_dec = sem("g_dec")
        g_zero_rows = sem("g_zero_rows")
        g_warm = sem("g_warm")
        v_veps = [sem(f"v_veps{n}") for n in range(5)]
        v_k0 = sem("v_k0")
        v_zeros = sem("v_zeros")
        a_warm = sem("a_warm")
        g_rstd = [sem(f"g_rstd{n}") for n in range(5)]

        pe_bias = sem("pe_bias")
        pe_bcont = sem("pe_bcont")
        pe_bdec = sem("pe_bdec")
        pe_xnT = sem("pe_xnT")
        pe_q = sem("pe_q")
        pe_k = sem("pe_k")
        pe_v = sem("pe_v")
        pe_s = sem("pe_s")
        pe_pT = sem("pe_pT")
        pe_o = sem("pe_o")
        pe_hT = sem("pe_hT")
        pe_enc = sem("pe_enc")
        pe_cont = sem("pe_cont")
        pe_logit = sem("pe_logit")
        pe_h = sem("pe_h")
        pe_y = sem("pe_y")
        pe_moeT = sem("pe_moeT")
        pe_c2s = sem("pe_c2s")
        pe_dec = sem("pe_dec")

        a_xnT = sem("a_xnT")
        a_q = sem("a_q")
        a_k = sem("a_k")
        a_exp = sem("a_exp")
        a_pT = sem("a_pT")
        a_hT = sem("a_hT")
        a_enc = sem("a_enc")
        a_hi = sem("a_hi")
        a_mhi = sem("a_mhi")
        a_e2 = sem("a_e2")
        a_h = sem("a_h")
        a_c2s = sem("a_c2s")

        v_bias = sem("v_bias")
        v_bias2 = sem("v_bias2")
        v_bcont = sem("v_bcont")
        v_w1 = sem("v_w1")
        v_c2s = sem("v_c2s")
        v_b2 = sem("v_b2")
        v_bdec = sem("v_bdec")
        v_stats = [sem(f"v_stats{n}") for n in range(5)]
        v_mv = [sem(f"v_mv{n}") for n in range(5)]
        v_xn = sem("v_xn")
        v_v = sem("v_v")
        v_max = sem("v_max")
        v_epst = sem("v_epst")
        v_attn = sem("v_attn")
        v_hn = sem("v_hn")
        v_mid = sem("v_mid")
        v_cont = sem("v_cont")
        v_router = sem("v_router")
        v_prod = sem("v_prod")
        v_logit = sem("v_logit")
        v_top = sem("v_top")
        v_topno = sem("v_topno")
        v_diff = sem("v_diff")
        v_gate = sem("v_gate")
        v_gated = sem("v_gated")
        v_moe = sem("v_moe")
        v_moe2 = sem("v_moe2")
        v_mparts = sem("v_mparts")
        v_z1 = sem("v_z1")
        v_z = sem("v_z")
        v_zn = sem("v_zn")
        v_out = sem("v_out")

        block = ctx.enter_context(nc.Block())

        @block.sync
        def _(sp):
            def row(vec, n=1):
                return vec.rearrange("(a d) -> a d", a=n)

            sp.dma_start(x_in[:, 0], x_dram[0]).then_inc(d_x[0], 16)
            sp.dma_start(wq[:, :], Wq).then_inc(d_qkv, 16)
            sp.dma_start(bias_rows[R_Q:R_Q + 1, :], row(bq)).then_inc(d_rows, 16)
            sp.dma_start(bias_rows[R_K:R_K + 1, :], row(bk)).then_inc(d_rows, 16)
            sp.dma_start(wk[:, :], Wk).then_inc(d_qkv, 16)
            sp.dma_start(bias_rows[R_ENC:R_ENC + HC, :], row(b_enc, HC)).then_inc(d_rows, 16)
            sp.dma_start(bias_rows[R_C2S:R_C2S + HC, :], row(b_c2s, HC)).then_inc(d_rows, 16)
            sp.dma_start(bias_rows[R_B1:R_B1 + E, :], b1).then_inc(d_rows, 16)
            for half in range(2):
                sp.dma_start(bias_rows[R_S2C:R_S2C + 1, half * M:(half + 1) * M], row(b_s2c)).then_inc(d_rows, 16)
            sp.dma_start(wv[:, :], Wv).then_inc(d_qkv, 16)
            sp.dma_start(bv_all[:, :], bv.partition_broadcast(P)).then_inc(d_qkv, 16)
            sp.dma_start(x_in[:, 1], x_dram[1]).then_inc(d_x[1], 16)
            sp.dma_start(w_s2c_raw[:, :, :], W_s2c.rearrange("(c p) m -> p c m", p=P)).then_inc(d_s2c, 16)
            for half in range(2):
                sp.dma_start(w1_raw[half * M:(half + 1) * M], W1.rearrange("e m h -> m e h")).then_inc(d_w1, 16)
            sp.dma_start(w_enc[:, :], W_enc).then_inc(d_enc, 16)
            for half in range(2):
                sp.dma_start(w_r_raw[half * M:(half + 1) * M], Wr).then_inc(d_router, 16)
            sp.dma_start(br_all[:, :], br.partition_broadcast(P)).then_inc(d_router, 16)
            sp.dma_start(b2_all[:, :], b2.rearrange("e m -> (e m)").partition_broadcast(P)).then_inc(d_b2, 16)
            sp.dma_start(w2[:, :, :], W2.rearrange("e h m -> h e m")).then_inc(d_w2, 16)
            sp.dma_start(w_dec_raw[:, :, :], W_dec.rearrange("(c p) d -> p c d", p=P)).then_inc(d_dec, 16)
            sp.dma_start(b_dec_row[:, :], row(b_dec)).then_inc(d_dec, 16)
            for half in range(2):
                sp.dma_start(w_c2s_raw[half * M:(half + 1) * M], W_c2s).then_inc(d_c2s, 16)
            sp.dma_start(x_in[:, 2], x_dram[2]).then_inc(d_x[2], 16)
            sp.dma_start(g_all[:, :], ln_g.partition_broadcast(P)).then_inc(d_ln, 16)
            sp.dma_start(b_all[:, :], ln_b.partition_broadcast(P)).then_inc(d_ln, 16)
            sp.dma_start(x_in[:, 3], x_dram[3]).then_inc(d_x[3], 16)
            for b in range(B):
                for i, (t0, t1) in enumerate(parts(LN_Z, b)):
                    sp.wait_ge(v_out, parts_done(LN_Z, b, i))
                    sp.dma_start(out_dram[b, :, t0:t1], x_out[:, b, t0:t1]).then_inc(d_out, 16)
            sp.wait_ge(d_out, 16 * parts_done(LN_Z, B - 1, 1))

        @block.gpsimd
        def _(pool):
            nc.gpsimd.memset(ident[:, :], 0.0).then_inc(g_zero, 1)
            nc.gpsimd.memset(warm[:, :], 0.0).then_inc(g_warm, 1)
            nc.gpsimd.memset(minus_half[:, :], -0.5).then_inc(g_const, 1)
            pool.wait_ge(g_zero, 1)
            nc.gpsimd.affine_select(out=ident[:, :], in_=ident[:, :], compare_op=ALU.not_equal, fill=1.0, base=0,
                                    pattern=[[-1, P]], channel_multiplier=1).then_inc(g_const, 1)

            def inverse_std(n, b, i):
                t0, t1 = parts(n, b)[i]
                part = (slice(None), n, b % 2, slice(t0, t1))
                pool.wait_ge(v_veps[n], parts_done(n, b, i))
                nc.gpsimd.tensor_tensor(rstd[part], var_eps[part], minus_half[:, t0:t1], ALU.pow).then_inc(g_rstd[n], 1)

            pool.wait_ge(g_const, 2)
            for h in range(2):
                inverse_std(LN_X, 0, h)
            nc.gpsimd.memset(ones[:, :], 1.0).then_inc(g_const, 1)
            nc.gpsimd.memset(ones_bf[:, :], 1.0).then_inc(g_const, 1)
            for h in range(2):
                inverse_std(LN_X, 1, h)
            pool.wait_ge(d_s2c, 16)
            for half in range(2):
                nc.gpsimd.tensor_scalar(w_s2c[:, :, half], w_s2c_raw[:, :, :], 0.5, None, ALU.mult).then_inc(g_s2c, 1)
            nc.gpsimd.memset(b_dec_stack[:, :], 0.0).then_inc(g_zero_rows, 1)
            nc.gpsimd.memset(b2_stack[:, :], 0.0).then_inc(g_zero_rows, 1)
            for e in range(E):
                nc.gpsimd.memset(expert_no[:, e:e + 1], float(e)).then_inc(g_const, 1)
            pool.wait_ge(d_dec, 32)
            nc.gpsimd.tensor_scalar(w_dec[:, :, :], w_dec_raw[:, :, :], 0.5, None, ALU.mult).then_inc(g_dec, 1)
            for h in range(2):
                inverse_std(LN_ATT, 0, h)
                inverse_std(LN_MID, 0, h)
            for b in range(B):
                if b + 2 < B:
                    inverse_std(LN_X, b + 2, 0)
                if b >= 1:
                    inverse_std(LN_DEC, b - 1, 0)
                    inverse_std(LN_Z, b - 1, 0)
                for h in range(2 if b + 1 < B else 0):
                    inverse_std(LN_ATT, b + 1, h)
                    inverse_std(LN_MID, b + 1, h)
            for h in range(2):
                inverse_std(LN_DEC, B - 1, h)
                inverse_std(LN_Z, B - 1, h)

        @block.scalar
        def _(act):
            def xnT_out(b):
                act.wait_ge(pe_xnT, b + 1)
                nc.scalar.activation(xnT[:, b % 2], ps_a[:, :], ACT.Identity).then_inc(a_xnT, 1)

            def q_out(b):
                act.wait_ge(pe_q, b + 1)
                nc.scalar.activation(qT[:, b % 2], ps_a[:, :], ACT.Identity, bias=bq_scaled[:, :],
                                     scale=SCALE).then_inc(a_q, 1)

            def k_out(b):
                act.wait_ge(pe_k, b + 1)
                nc.scalar.activation(kT[:, b % 2], ps_a[:, :], ACT.Identity,
                                     bias=bias_cols[:, R_K:R_K + 1]).then_inc(a_k, 1)

            def exps(b, t):
                act.wait_ge(v_max, T * b + t + 1)
                nc.scalar.activation(probs[:, b % 2, t], ps_s[t % 2][:, :], ACT.Exp, bias=neg_max[:, b % 2, t:t + 1],
                                     accum_out=prob_sum[:, b % 2, t:t + 1]).then_inc(a_exp, 1)

            def pT_out(b, t):
                act.wait_ge(pe_pT, T * b + t + 1)
                nc.scalar.activation(probsT[:, b % 2, t], ps_t[:, :].rearrange("p (k q) -> p k q", k=T),
                                     ACT.Identity).then_inc(a_pT, 1)

            def hT_out(b):
                act.wait_ge(pe_hT, b + 1)
                nc.scalar.activation(hT[:, b % 2], turned_bank(b)[:, :], ACT.Identity).then_inc(a_hT, 1)

            def encode(b, c):
                act.wait_ge(pe_enc, HC * b + c + 1)
                nc.scalar.activation(spikes[:, b % 2, c], encode_bank(b, c)[:, :], ACT.Tanh,
                                     bias=bias_half[:, c:c + 1], scale=0.5).then_inc(a_enc, 1)

            def cont_out(b):
                act.wait_ge(pe_cont, b + 1)
                if b == 0:
                    act.wait_ge(v_bcont, 1)
                nc.scalar.activation(cont_parts[:, b % 2], slot(F_CONT)[:, :], ACT.Identity,
                                     bias=b_cont[:, :]).then_inc(a_hi, 1)

            def moe_out(b):
                act.wait_ge(pe_moeT, b + 1)
                nc.scalar.activation(moe_parts[:, b % 2], slot(F_MT)[:, :], ACT.Identity).then_inc(a_mhi, 1)

            def second_exp(b):
                act.wait_ge(v_diff, b + 1)
                nc.scalar.activation(e2[:, b % 2], top_diff[:, b % 2], ACT.Exp).then_inc(a_e2, 1)

            def relu(b, e):
                act.wait_ge(pe_h, E * b + e + 1)
                if e == 0 and b >= 1:
                    act.wait_ge(pe_y, T * b)
                nc.scalar.activation(hidden[:, e], hidden_bank(b, e)[:, :], ACT.Relu,
                                     bias=bias_cols[:, R_B1 + e:R_B1 + e + 1]).then_inc(a_h, 1)

            def spike(b, c):
                act.wait_ge(pe_c2s, HC * b + c + 1)
                nc.scalar.activation(spikes2[:, b % 2, c], slot(F_C2S[c])[:, :], ACT.Tanh,
                                     bias=bias_half[:, HC + c:HC + c + 1], scale=0.5).then_inc(a_c2s, 1)

            def last_moe_out(h):
                act.wait_ge(pe_moeT, B + h)
                t0, t1 = LAST[h]
                part = slice(t0 * P, t1 * P)
                nc.scalar.activation(moe_parts[:, (B - 1) % 2, part], last_moeT[h][:, part],
                                     ACT.Identity).then_inc(a_mhi, 1)

            def last_spike(c, h):
                act.wait_ge(pe_c2s, HC * (B - 1) + HC * h + c + 1)
                t0, t1 = LAST[h]
                part = slice(t0 * P, t1 * P)
                nc.scalar.activation(spikes2[:, (B - 1) % 2, c, part], last_c2s[h][c][:, part], ACT.Tanh,
                                     bias=bias_half[:, HC + c:HC + c + 1], scale=0.5).then_inc(a_c2s, 1)

            act.wait_ge(g_warm, 1)
            nc.scalar.activation(warm[:, :], warm[:, :], ACT.Exp).then_inc(a_warm, 1)
            xnT_out(0)
            act.wait_ge(v_bias2, 3)
            q_out(0)
            exps(0, 0)
            xnT_out(1)
            pT_out(0, 0)
            exps(0, 1)
            q_out(1)
            for t in range(1, T):
                if t == T - 1:
                    k_out(1)
                pT_out(0, t)
                if t + 1 < T:
                    exps(0, t + 1)
            exps(1, 0)
            pT_out(1, 0)
            hT_out(0)
            exps(1, 1)
            encode(0, 0)
            exps(1, 2)
            encode(0, 1)
            pT_out(1, 1)
            cont_out(0)
            pT_out(1, 2)
            exps(1, 3)
            for b in range(B):
                n, m = b + 1, b + 2
                more, more2 = n < B, m < B
                first = more and b >= 1
                relu(b, 0)
                if first:
                    pT_out(n, 0)
                    exps(n, 1)
                relu(b, 1)
                relu(b, 2)
                second_exp(b)
                if first:
                    pT_out(n, 1)
                    exps(n, 2)
                relu(b, 3)
                relu(b, 4)
                if first:
                    pT_out(n, 2)
                    exps(n, 3)
                relu(b, 5)
                if more and not more2:
                    pT_out(n, 3)
                relu(b, 6)
                if more2:
                    pT_out(n, 3)
                relu(b, 7)
                if more2:
                    xnT_out(m)
                    q_out(m)
                    k_out(m)
                if more:
                    hT_out(n)
                if more:
                    encode(n, 0)
                    if more2:
                        moe_out(b)
                    encode(n, 1)
                    if not more2:
                        moe_out(b)
                        cont_out(n)
                    for c in range(HC):
                        spike(b, c)
                if more2:
                    exps(m, 0)
                    cont_out(n)
            for h in range(2):
                last_moe_out(h)
                for c in range(HC):
                    last_spike(c, h)

        @block.tensor
        def _(pe):
            def turn_x(b):
                pe.wait_ge(v_xn, T * (b + 1))
                if b == 0:
                    pe.wait_ge(g_const, 2)
                elif b == 1:
                    pe.wait_ge(a_q, 1)
                else:
                    pe.wait_ge(v_attn, T * (b - 1) + TH)
                for t in range(T):
                    mm = nc.tensor.transpose(ps_a[:, t * P:(t + 1) * P], xn[:, b % 2, t], ident[:, :])
                mm.then_inc(pe_xnT, 1)

            def project_q(b):
                pe.wait_ge(a_xnT, b + 1)
                if b == 0:
                    pe.wait_ge(d_qkv, 64)
                nc.tensor.matmul(ps_a[:, :], wq[:, :], xnT[:, b % 2], start=True, stop=True).then_inc(pe_q, 1)

            def project_k(b):
                if b >= 1:
                    pe.wait_ge(a_q, b + 1)
                nc.tensor.matmul((ps_a if b else ps_s[1])[:, :], wk[:, :], xnT[:, b % 2],
                                 start=True, stop=True).then_inc(pe_k, 1)

            def project_v(b):
                if b >= 1:
                    pe.wait_ge(a_k, b)
                for t in range(T):
                    mm = nc.tensor.matmul((ps_a if b else ps_t)[:, t * P:(t + 1) * P],
                                          xnT[:, b % 2, t * P:(t + 1) * P], wv[:, :], start=True, stop=True)
                mm.then_inc(pe_v, 1)

            def scores(b, t):
                if t == 0 and b == 0:
                    pe.wait_ge(a_q, 1)
                    pe.wait_ge(v_k0, 1)
                elif t == 0:
                    pe.wait_ge(a_k, b)
                if T * b + t >= 2:
                    pe.wait_ge(a_exp, T * b + t - 1)
                nc.tensor.matmul(ps_s[t % 2][:, :], qT[:, b % 2, t * P:(t + 1) * P], kT[:, b % 2],
                                 start=True, stop=True).then_inc(pe_s, 1)

            def turn_probs(b, t):
                pe.wait_ge(a_exp, T * b + t + 1)
                if T * b + t >= 1:
                    pe.wait_ge(a_pT, T * b + t)
                else:
                    pe.wait_ge(v_v, 1)
                for k in range(T):
                    mm = nc.tensor.transpose(ps_t[:, k * P:(k + 1) * P], probs[:, b % 2, t, k * P:(k + 1) * P],
                                             ident[:, :])
                mm.then_inc(pe_pT, 1)

            def attend(b, t):
                pe.wait_ge(a_pT, T * b + t + 1)
                if t == 0:
                    pe.wait_ge(v_v, b + 1)
                if t == TH and b >= 1:
                    pe.wait_ge(v_attn, T * b)
                if t == TH and b == 0:
                    pe.wait_ge(v_bcont, 1)
                for k in range(T):
                    mm = nc.tensor.matmul(attn_out(b, t), probsT[:, b % 2, t, k], v[:, b % 2, k],
                                          start=(k == 0), stop=(k == T - 1))
                if t % TH == TH - 1:
                    mm.then_inc(pe_o, 1)

            def turn_h(b):
                pe.wait_ge(v_hn, T * (b + 1))
                if 1 <= b < B - 1:
                    pe.wait_ge(v_gated, T * b - 2)
                for t in range(T):
                    mm = nc.tensor.transpose(turned_bank(b)[:, t * P:(t + 1) * P], hn[:, b % 2, t], ident[:, :])
                mm.then_inc(pe_hT, 1)

            def encode(b, c):
                pe.wait_ge(a_hT, b + 1)
                if b == 0:
                    pe.wait_ge(d_enc, 16)
                    pe.wait_ge(v_bdec, 2)
                elif b < B - 1:
                    pe.wait_ge(v_gated, T * b - 1)
                nc.tensor.matmul(encode_bank(b, c)[:, :], w_enc[:, c * P:(c + 1) * P], hT[:, b % 2],
                                 start=True, stop=True).then_inc(pe_enc, 1)

            def to_cont(b):
                pe.wait_ge(a_enc, HC * (b + 1))
                if b == 0:
                    pe.wait_ge(g_s2c, 2)
                for c in range(HC):
                    mm = nc.tensor.matmul(slot(F_CONT)[:, :], w_s2c[:, c], spikes[:, b % 2, c],
                                          start=(c == 0), stop=(c == HC - 1))
                mm.then_inc(pe_cont, 1)

            def route(b):
                pe.wait_ge(v_cont, b + 1)
                if b == 0:
                    pe.wait_ge(v_router, 2)
                elif b < B - 1:
                    pe.wait_ge(a_c2s, HC * b)
                for t in range(T):
                    mm = nc.tensor.matmul(logit_bank(b)[:, 2 * t * E:2 * (t + 1) * E],
                                          cont_parts[:, b % 2, t * P:(t + 1) * P],
                                          w_r[:, :, :].rearrange("p a e -> p (a e)"), start=True, stop=True)
                mm.then_inc(pe_logit, 1)

            def hidden_units(b, e):
                if e == 0:
                    pe.wait_ge(v_cont, b + 1)
                    if b == 0:
                        pe.wait_ge(v_w1, 2)
                if e == 1 and 1 <= b < B - 1:
                    pe.wait_ge(v_z1, T * b)
                if e == 2 and b < B - 1:
                    pe.wait_ge(v_prod, b + 1)
                if e >= 3:
                    pe.wait_ge(a_h, E * b + e - 2)
                bank = hidden_bank(b, e)
                nc.tensor.matmul(bank[:, :], w1_hi[:, e], cont_parts[:, b % 2], start=True, stop=False)
                nc.tensor.matmul(bank[:, :], w1_lo[:, e], cont_parts[:, b % 2], start=False,
                                 stop=True).then_inc(pe_h, 1)

            def expert_out(b, t):
                if t == 0:
                    if b == 0:
                        pe.wait_ge(d_w2, 16)
                        pe.wait_ge(v_b2, 6)
                if t == T - 1:
                    pe.wait_ge(v_gated, T * b + 1)
                if t == 2 and b == B - 1:
                    pe.wait_ge(v_z1, T * b)
                if t < T - 1:
                    pe.wait_ge(a_h, E * b + E - 2 + t)
                y = slot(F_Y + t)
                nc.tensor.matmul(y[:, :], ones_bf[:, :], b2_stack[:, :], start=True, stop=False)
                for e in range(E):
                    if t == 0:
                        pe.wait_ge(a_h, E * b + e + 1)
                    mm = nc.tensor.matmul(y[:, e * M:(e + 1) * M], hidden[:, e, t * P:(t + 1) * P], w2[:, e],
                                          start=False, stop=(e == E - 1))
                mm.then_inc(pe_y, 1)

            def turn_moe(b):
                pe.wait_ge(v_moe2, T * (b + 1))
                for t in range(T):
                    mm = nc.tensor.transpose(slot(F_MT)[:, t * P:(t + 1) * P],
                                             moe[:, b % 2, t].rearrange("p a m -> p (a m)"), ident[:, :])
                mm.then_inc(pe_moeT, 1)

            def to_spikes(b, c):
                pe.wait_ge(v_mparts, b + 1)
                if b + 1 < B:
                    pe.wait_ge(a_enc, HC * (b + 1) + 1)
                if b == 0:
                    pe.wait_ge(v_c2s, 2)
                nc.tensor.matmul(slot(F_C2S[c])[:, :], w_c2s_hi[:, c * P:(c + 1) * P], moe_parts[:, b % 2],
                                 start=True, stop=False)
                nc.tensor.matmul(slot(F_C2S[c])[:, :], w_c2s_lo[:, c * P:(c + 1) * P], moe_parts[:, b % 2],
                                 start=False, stop=True).then_inc(pe_c2s, 1)

            def decode(b):
                pe.wait_ge(a_c2s, HC * (b + 1))
                if b == 0:
                    pe.wait_ge(v_bdec, 8)
                for t in range(T):
                    d = slot(F_DEC)[:, t * P:(t + 1) * P]
                    nc.tensor.matmul(d, ones_bf[:, :], b_dec_stack[:, :], start=True, stop=False)
                    for c in range(HC):
                        mm = nc.tensor.matmul(d, spikes2[:, b % 2, c, t * P:(t + 1) * P], w_dec[:, c],
                                              start=False, stop=(c == HC - 1))
                mm.then_inc(pe_dec, 1)

            def turn_last_moe(h):
                t0, t1 = LAST[h]
                pe.wait_ge(v_moe2, T * (B - 1) + t1)
                for t in range(t0, t1):
                    mm = nc.tensor.transpose(last_moeT[h][:, t * P:(t + 1) * P],
                                             moe[:, (B - 1) % 2, t].rearrange("p a m -> p (a m)"), ident[:, :])
                mm.then_inc(pe_moeT, 1)

            def last_to_spikes(c, h):
                t0, t1 = LAST[h]
                part = slice(t0 * P, t1 * P)
                pe.wait_ge(v_mparts, B + h)
                for weights, start in ((w_c2s_hi, True), (w_c2s_lo, False)):
                    mm = nc.tensor.matmul(last_c2s[h][c][:, part], weights[:, c * P:(c + 1) * P],
                                          moe_parts[:, (B - 1) % 2, part], start=start, stop=not start)
                mm.then_inc(pe_c2s, 1)

            def decode_last(h):
                pe.wait_ge(a_c2s, HC * (B - 1) + HC * (h + 1))
                for t in range(*LAST[h]):
                    d = last_dec[h][:, t * P:(t + 1) * P]
                    nc.tensor.matmul(d, ones_bf[:, :], b_dec_stack[:, :], start=True, stop=False)
                    for c in range(HC):
                        mm = nc.tensor.matmul(d, spikes2[:, (B - 1) % 2, c, t * P:(t + 1) * P], w_dec[:, c],
                                              start=False, stop=(c == HC - 1))
                mm.then_inc(pe_dec, 1)

            pe.wait_ge(v_zeros, 1)
            for _ in range(WARM_UP):
                nc.tensor.matmul(ps_t[:, :], zeros[:, 0:P], zeros[:, :], start=True, stop=True)
            turn_x(0)
            pe.wait_ge(d_rows, 16 * 7)
            nc.tensor.transpose(ps_o[:, 0:ROWS], bias_rows[:, :], ident[0:ROWS, 0:ROWS]).then_inc(pe_bias, 1)
            project_q(0)
            project_k(0)
            project_v(0)
            scores(0, 0)
            scores(0, 1)
            turn_x(1)
            turn_probs(0, 0)
            pe.wait_ge(g_s2c, 2)
            pe.wait_ge(g_const, 4)
            pe.wait_ge(v_bias, 1)
            for c in range(HC):
                mm = nc.tensor.matmul(ps_o[:, 0:1], w_s2c[:, c], ones[:, 0:1], start=(c == 0), stop=(c == HC - 1))
            mm.then_inc(pe_bcont, 1)
            scores(0, 2)
            project_q(1)
            attend(0, 0)
            turn_probs(0, 1)
            scores(0, 3)
            attend(0, 1)
            turn_probs(0, 2)
            project_k(1)
            attend(0, 2)
            turn_probs(0, 3)
            project_v(1)
            attend(0, 3)
            scores(1, 0)
            scores(1, 1)
            pe.wait_ge(g_dec, 1)
            for c in range(HC):
                nc.tensor.matmul(slot(F_ENC[0])[:, 0:D], ones[:, :], w_dec[:, c], start=(c == 0), stop=False)
            nc.tensor.matmul(slot(F_ENC[0])[:, 0:D], ones[0:1, :], b_dec_row[:, :], start=False,
                             stop=True).then_inc(pe_bdec, 1)
            turn_probs(1, 0)
            scores(1, 2)
            turn_h(0)
            attend(1, 0)
            encode(0, 0)
            encode(0, 1)
            turn_probs(1, 1)
            to_cont(0)
            scores(1, 3)
            attend(1, 1)
            turn_probs(1, 2)
            route(0)
            for b in range(B):
                n, m = b + 1, b + 2
                more, more2 = n < B, m < B
                first = more and b >= 1
                if more:
                    hidden_units(b, 0)
                if first:
                    turn_probs(n, 0)
                    scores(n, 2)
                if more:
                    hidden_units(b, 1)
                    hidden_units(b, 2)
                if first:
                    attend(n, 0)
                    turn_probs(n, 1)
                hidden_units(b, 3)
                hidden_units(b, 4)
                if first:
                    scores(n, 3)
                    attend(n, 1)
                    turn_probs(n, 2)
                hidden_units(b, 5)
                hidden_units(b, 6)
                if more:
                    attend(n, 2)
                    turn_probs(n, 3)
                hidden_units(b, 7)
                if more and not more2:
                    attend(n, 3)
                expert_out(b, 0)
                if more2:
                    attend(n, 3)
                if more2:
                    turn_x(m)
                expert_out(b, 1)
                if more2:
                    project_q(m)
                expert_out(b, 2)
                if more2:
                    project_k(m)
                if not more:
                    break
                expert_out(b, 3)
                turn_h(n)
                if more2:
                    project_v(m)
                encode(n, 0)
                if more2:
                    turn_moe(b)
                encode(n, 1)
                if more2:
                    scores(m, 0)
                else:
                    turn_moe(b)
                    to_cont(n)
                for c in range(HC):
                    to_spikes(b, c)
                if more2:
                    to_cont(n)
                    decode(b)
                    route(n)
                    scores(m, 1)
                else:
                    route(n)
                    for e in range(3):
                        hidden_units(n, e)
                    decode(b)
            turn_last_moe(0)
            expert_out(B - 1, T - 1)
            for c in range(HC):
                last_to_spikes(c, 0)
            turn_last_moe(1)
            decode_last(0)
            for c in range(HC):
                last_to_spikes(c, 1)
            decode_last(1)

        @block.vector
        def _(dve):
            def statistics(n, b, i, source):
                t0, t1 = parts(n, b)[i]
                part = slice(t0, t1)
                for t in range(t0, t1):
                    nc.vector.bn_stats(stats[:, n, b % 2, t], source(t)).then_inc(v_stats[n], 1)
                for t in range(t0, t1):
                    dve.wait_ge(v_stats[n], T * b + t + 1)
                    nc.vector.bn_aggr(mean_var[:, n, b % 2, t], stats[:, n, b % 2, t]).then_inc(v_mv[n], 1)
                dve.wait_ge(v_mv[n], T * b + t1)
                if n == LN_ATT:
                    nc.vector.tensor_tensor(var_eps[:, n, b % 2, part], mean_var[:, n, b % 2, part, 1],
                                            eps_term[:, b % 2, part], ALU.add).then_inc(v_veps[n], 1)
                else:
                    nc.vector.tensor_scalar(var_eps[:, n, b % 2, part], mean_var[:, n, b % 2, part, 1], EPS, None,
                                            ALU.add).then_inc(v_veps[n], 1)

            def normed(n, b, i, source, result, done):
                t0, t1 = parts(n, b)[i]
                dve.wait_ge(g_rstd[n], parts_done(n, b, i))
                for t in range(t0, t1):
                    nc.vector.tensor_scalar(result(t), source(t), mean(n, b, t), inv(n, b, t), ALU.subtract,
                                            ALU.mult).then_inc(done, 1)

            def mean(n, b, t):
                return mean_var[:, n, b % 2, t, 0:1]

            def inv(n, b, t):
                return rstd[:, n, b % 2, t:t + 1]

            def x_stats(b):
                dve.wait_ge(d_x[b], 16)
                for i in range(len(parts(LN_X, b))):
                    statistics(LN_X, b, i, lambda t: x_in[:, b, t])

            def x_norm(b):
                for i in range(len(parts(LN_X, b))):
                    normed(LN_X, b, i, lambda t: x_in[:, b, t], lambda t: xn[:, b % 2, t], v_xn)

            def add_bv(b):
                dve.wait_ge(pe_v, b + 1)
                nc.vector.tensor_tensor(v[:, b % 2], (ps_a if b else ps_t)[:, :].rearrange("p (t d) -> p t d", t=T),
                                        bv_all[:, :].unsqueeze(1).to_broadcast([P, T, D]), ALU.add).then_inc(v_v, 1)

            def row_max(b, t):
                dve.wait_ge(pe_s, T * b + t + 1)
                nc.vector.tensor_reduce(neg_max[:, b % 2, t:t + 1], ps_s[t % 2][:, :], AX_X, ALU.max,
                                        negate=True).then_inc(v_max, 1)

            def attn_stats(b, h):
                dve.wait_ge(a_exp, T * b + TH * (h + 1))
                part = slice(TH * h, TH * (h + 1))
                nc.vector.scalar_tensor_tensor(eps_term[:, b % 2, part], prob_sum[:, b % 2, part], EPS,
                                               prob_sum[:, b % 2, part], ALU.mult, ALU.mult).then_inc(v_epst, 1)
                dve.wait_ge(v_epst, 2 * b + h + 1)
                dve.wait_ge(pe_o, 2 * b + h + 1)
                statistics(LN_ATT, b, h, lambda t: attn_out(b, t))

            def mid_stats(b, h):
                normed(LN_ATT, b, h, lambda t: attn_out(b, t), lambda t: attn[:, b % 2, t], v_attn)
                dve.wait_ge(v_attn, T * b + TH * (h + 1))
                part = slice(TH * h, TH * (h + 1))
                nc.vector.tensor_tensor(x_mid[:, b, part], attn[:, b % 2, part], x_in[:, b, part],
                                        ALU.add).then_inc(v_mid, 1)
                dve.wait_ge(v_mid, 2 * b + h + 1)
                statistics(LN_MID, b, h, lambda t: x_mid[:, b, t])

            def mid_norm(b, h):
                normed(LN_MID, b, h, lambda t: x_mid[:, b, t], lambda t: hn[:, b % 2, t], v_hn)

            def split_cont(b):
                dve.wait_ge(a_hi, b + 1)
                nc.vector.scalar_tensor_tensor(cont_parts[M:P, b % 2], slot(F_CONT)[M:P, :], b_cont[M:P, :],
                                               cont_parts[M:P, b % 2].bitcast(F32), ALU.add,
                                               ALU.subtract).then_inc(v_cont, 1)

            def router_top(b):
                i = b % 2
                dve.wait_ge(pe_logit, b + 1)
                nc.vector.tensor_reduce(products[:, i], logit_bank(b)[:, 0:2 * T * E].rearrange(
                    "p (t a e) -> p t e a", t=T, a=2), AX_X, ALU.add).then_inc(v_prod, 1)
                dve.wait_ge(v_prod, b + 1)
                nc.vector.tensor_tensor(logits[:, i], products[:, i], br_all[:, :].unsqueeze(1).to_broadcast([P, T, E]),
                                        ALU.add).then_inc(v_logit, 1)
                dve.wait_ge(v_logit, b + 1)
                for t in range(T):
                    nc.vector.max(top[:, i, t], logits[:, i, t]).then_inc(v_top, 1)
                for t in range(T):
                    dve.wait_ge(v_top, T * b + t + 1)
                    nc.vector.max_index(top_no[:, i, t], top[:, i, t], logits[:, i, t]).then_inc(v_topno, 1)
                nc.vector.tensor_tensor(top_diff[:, i], top[:, i, :, 1], top[:, i, :, 0],
                                        ALU.subtract).then_inc(v_diff, 1)

            def router_gates(b):
                i = b % 2

                def wide(w):
                    return w[:, i].unsqueeze(2).to_broadcast([P, T, E])

                count = 9 * b
                dve.wait_ge(v_topno, T * (b + 1))
                for pick, j in ((pick1, 0), (pick2, 1)):
                    nc.vector.tensor_tensor(pick[:, i], expert_no[:, :].unsqueeze(1).to_broadcast([P, T, E]),
                                            top_no[:, i, :, j:j + 1].to_broadcast([P, T, E]),
                                            ALU.is_equal).then_inc(v_gate, 1)
                dve.wait_ge(a_e2, b + 1)
                nc.vector.tensor_scalar(e_sum[:, i], e2[:, i], 1.0, None, ALU.add).then_inc(v_gate, 1)
                dve.wait_ge(v_gate, count + 3)
                nc.vector.reciprocal(w_first[:, i], e_sum[:, i]).then_inc(v_gate, 1)
                dve.wait_ge(v_gate, count + 4)
                nc.vector.tensor_tensor(w_second[:, i], e2[:, i], w_first[:, i], ALU.mult).then_inc(v_gate, 1)
                nc.vector.tensor_tensor(pick1[:, i], pick1[:, i], wide(w_first), ALU.mult).then_inc(v_gate, 1)
                dve.wait_ge(v_gate, count + 5)
                nc.vector.tensor_tensor(pick2[:, i], pick2[:, i], wide(w_second), ALU.mult).then_inc(v_gate, 1)
                dve.wait_ge(v_gate, count + 7)
                nc.vector.tensor_tensor(gate[:, i], pick1[:, i], pick2[:, i], ALU.add).then_inc(v_gate, 2)

            def double(b, t):
                dve.wait_ge(v_moe, T * b + t + 1)
                nc.vector.tensor_copy(moe[:, b % 2, t, 1], moe[:, b % 2, t, 0]).then_inc(v_moe2, 1)

            def apply_gates(b, t):
                n = T * b + t
                dve.wait_ge(pe_y, n + 1)
                dve.wait_ge(v_gate, 9 * (b + 1))
                if n >= 2:
                    dve.wait_ge(v_moe, n - 1)
                nc.vector.tensor_tensor(gated[:, n % 2], slot(F_Y + t)[:, :].rearrange("p (e m) -> p e m", e=E),
                                        gate[:, b % 2, t].unsqueeze(2).to_broadcast([P, E, M]),
                                        ALU.mult).then_inc(v_gated, 1)

            def sum_experts(b, t):
                n = T * b + t
                ends_part = [t1 - 1 for _, t1 in LAST] if b == B - 1 else [T - 1]
                if t >= 1 and t - 1 not in ends_part:
                    double(b, t - 1)
                dve.wait_ge(v_gated, n + 1)
                nc.vector.tensor_reduce(moe[:, b % 2, t, 0], gated[:, n % 2].rearrange("p e m -> p m e"), AX_X,
                                        ALU.add).then_inc(v_moe, 1)
                if t in ends_part:
                    double(b, t)

            def combine(b, t):
                apply_gates(b, t)
                sum_experts(b, t)

            def split_last_moe(h):
                t0, t1 = LAST[h]
                part = slice(t0 * P, t1 * P)
                i = (B - 1) % 2
                dve.wait_ge(a_mhi, B + h)
                nc.vector.tensor_tensor(moe_parts[M:P, i, part], last_moeT[h][M:P, part],
                                        moe_parts[M:P, i, part].bitcast(F32), ALU.subtract).then_inc(v_mparts, 1)

            def split_moe(b):
                dve.wait_ge(a_mhi, b + 1)
                nc.vector.tensor_tensor(moe_parts[M:P, b % 2], slot(F_MT)[M:P, :],
                                        moe_parts[M:P, b % 2].bitcast(F32), ALU.subtract).then_inc(v_mparts, 1)

            def decoded(b, t):
                return (last_dec[t >= LAST[1][0]] if b == B - 1 else slot(F_DEC))[:, t * P:(t + 1) * P]

            def dec_stats(b, i):
                dve.wait_ge(pe_dec, parts_done(LN_DEC, b, i))
                statistics(LN_DEC, b, i, lambda t: decoded(b, t))

            def dec_scale(b, i):
                for t in range(*parts(LN_DEC, b)[i]):
                    nc.vector.scalar_tensor_tensor(z1[:, b % 2, t], decoded(b, t), mean(LN_DEC, b, t), g_all[:, :],
                                                   ALU.subtract, ALU.mult).then_inc(v_z1, 1)

            def z_stats(b, i):
                dve.wait_ge(g_rstd[LN_DEC], parts_done(LN_DEC, b, i))
                t0, t1 = parts(LN_Z, b)[i]
                for t in range(t0, t1):
                    dve.wait_ge(v_z1, T * b + t + 1)
                    nc.vector.scalar_tensor_tensor(z[:, b % 2, t], z1[:, b % 2, t], inv(LN_DEC, b, t), b_all[:, :],
                                                   ALU.mult, ALU.add).then_inc(v_z, 1)
                dve.wait_ge(v_z, T * b + t1)
                statistics(LN_Z, b, i, lambda t: z[:, b % 2, t])

            def z_unit(b, i):
                normed(LN_Z, b, i, lambda t: z[:, b % 2, t], lambda t: zn[:, b % 2, t], v_zn)

            def z_add(b, i):
                t0, t1 = parts(LN_Z, b)[i]
                dve.wait_ge(v_zn, T * b + t1)
                nc.vector.tensor_tensor(x_out[:, b, t0:t1], zn[:, b % 2, t0:t1], x_mid[:, b, t0:t1],
                                        ALU.add).then_inc(v_out, 1)

            def z_norm(b, i):
                z_unit(b, i)
                z_add(b, i)

            nc.vector.memset(zeros[:, :], 0.0).then_inc(v_zeros, 1)
            x_stats(0)
            x_norm(0)
            dve.wait_ge(pe_bias, 1)
            nc.vector.tensor_copy(bias_cols[:, :], ps_o[:, 0:ROWS]).then_inc(v_bias, 1)
            dve.wait_ge(v_bias, 1)
            nc.vector.tensor_scalar(bq_scaled[:, :], bias_cols[:, R_Q:R_Q + 1], SCALE, None, ALU.mult).then_inc(v_bias2, 1)
            nc.vector.tensor_scalar(bias_half[:, 0:HC], bias_cols[:, R_ENC:R_ENC + HC], 0.5, None,
                                    ALU.mult).then_inc(v_bias2, 1)
            nc.vector.tensor_scalar(bias_half[:, HC:2 * HC], bias_cols[:, R_C2S:R_C2S + HC], 0.5, None,
                                    ALU.mult).then_inc(v_bias2, 1)
            x_stats(1)
            dve.wait_ge(pe_k, 1)
            nc.vector.tensor_scalar(kT[:, 0], ps_s[1][:, :], bias_cols[:, R_K:R_K + 1], None, ALU.add).then_inc(v_k0, 1)
            add_bv(0)
            x_norm(1)
            row_max(0, 0)
            row_max(0, 1)
            dve.wait_ge(pe_bcont, 1)
            nc.vector.tensor_tensor(b_cont[:, :], ps_o[:, 0:1], bias_cols[:, R_S2C:R_S2C + 1], ALU.add).then_inc(
                v_bcont, 1)
            row_max(0, 2)
            dve.wait_ge(d_w1, 32)
            nc.vector.tensor_copy(w1_hi[:, :, :], w1_raw[:, :, :]).then_inc(v_w1, 1)
            row_max(0, 3)
            attn_stats(0, 0)
            dve.wait_ge(v_w1, 1)
            nc.vector.tensor_tensor(w1_lo[:, :, :], w1_raw[:, :, :], w1_hi[:, :, :].bitcast(F32),
                                    ALU.subtract).then_inc(v_w1, 1)
            mid_stats(0, 0)
            attn_stats(0, 1)
            row_max(1, 0)
            mid_norm(0, 0)
            mid_stats(0, 1)
            add_bv(1)
            mid_norm(0, 1)

            def split_row(row, rest, hi, mid, stack, s, base):
                nc.vector.tensor_copy(hi, row).then_inc(s, 1)
                dve.wait_ge(s, base + 1)
                nc.vector.tensor_tensor(rest, row, hi, ALU.subtract).then_inc(s, 1)
                dve.wait_ge(s, base + 2)
                nc.vector.tensor_copy(mid, rest).then_inc(s, 1)
                dve.wait_ge(s, base + 3)
                nc.vector.tensor_copy(stack[0:1], hi[0:1]).then_inc(s, 1)
                nc.vector.tensor_copy(stack[32:33], mid[32:33]).then_inc(s, 1)
                nc.vector.tensor_tensor(stack[64:65], rest[64:65], mid[64:65], ALU.subtract).then_inc(s, 1)

            dve.wait_ge(pe_bdec, 1)
            nc.vector.tensor_copy(b_dec_sum[:, :], slot(F_ENC[0])[:, 0:D]).then_inc(v_bdec, 2)
            row_max(1, 1)
            row_max(1, 2)
            dve.wait_ge(d_b2, 16)
            dve.wait_ge(g_zero_rows, 2)
            split_row(b2_all[:, :], b2_rest[:, :], b2_hi[:, :], b2_mid[:, :], b2_stack[:, :], v_b2, 0)
            dve.wait_ge(v_bdec, 2)
            split_row(b_dec_sum[:, :], b_dec_rest[:, :], b_dec_hi[:, :], b_dec_mid[:, :], b_dec_stack[:, :], v_bdec, 2)
            dve.wait_ge(d_router, 48)
            nc.vector.tensor_copy(w_r[:, 0], w_r_raw[:, :]).then_inc(v_router, 1)
            dve.wait_ge(v_router, 1)
            nc.vector.tensor_tensor(w_r[:, 1], w_r_raw[:, :], w_r[:, 0].bitcast(F32), ALU.subtract).then_inc(v_router, 1)
            x_stats(2)
            split_cont(0)
            row_max(1, 3)
            x_norm(2)
            for b in range(B):
                n, m = b + 1, b + 2
                more, more2 = n < B, m < B
                first = more and b >= 1
                if b == 1:
                    dve.wait_ge(d_ln, 32)
                if b >= 1 and more:
                    dec_stats(b - 1, 0)
                    dec_scale(b - 1, 0)
                if first:
                    row_max(n, 1)
                router_top(b)
                if first:
                    row_max(n, 2)
                if not more:
                    router_gates(b)
                    dec_stats(b - 1, 0)
                    dec_scale(b - 1, 0)
                if b == 0:
                    dve.wait_ge(d_c2s, 32)
                    dve.wait_ge(g_const, 12)
                    nc.vector.tensor_copy(w_c2s_hi[:, :], w_c2s_raw[:, :]).then_inc(v_c2s, 1)
                    dve.wait_ge(v_c2s, 1)
                    nc.vector.tensor_tensor(w_c2s_lo[:, :], w_c2s_raw[:, :], w_c2s_hi[:, :].bitcast(F32),
                                            ALU.subtract).then_inc(v_c2s, 1)
                if b >= 1:
                    z_stats(b - 1, 0)
                if more:
                    router_gates(b)
                if first:
                    row_max(n, 3)
                if more:
                    attn_stats(n, 0)
                    if b >= 1 and more2:
                        z_norm(b - 1, 0)
                    mid_stats(n, 0)
                if more and not more2:
                    attn_stats(n, 1)
                    mid_norm(n, 0)
                    apply_gates(b, 0)
                else:
                    combine(b, 0)
                if more2:
                    attn_stats(n, 1)
                    mid_norm(n, 0)
                if more2:
                    combine(b, 1)
                    mid_stats(n, 1)
                    combine(b, 2)
                    mid_norm(n, 1)
                elif more:
                    mid_stats(n, 1)
                    sum_experts(b, 0)
                    mid_norm(n, 1)
                    combine(b, 1)
                    combine(b, 2)
                else:
                    for t in range(1, T - 1):
                        combine(b, t)
                        if t + 1 == LAST[0][1]:
                            split_last_moe(0)
                combine(b, 3)
                if more2:
                    add_bv(m)
                if more and not more2:
                    z_unit(b - 1, 0)
                if more:
                    split_moe(b)
                if more and not more2:
                    z_add(b - 1, 0)
                if m + 1 < B:
                    x_stats(m + 1)
                if more2:
                    row_max(m, 0)
                if m + 1 < B:
                    x_norm(m + 1)
                if more:
                    split_cont(n)
            z_unit(B - 2, 0)
            split_last_moe(1)
            z_add(B - 2, 0)
            dec_stats(B - 1, 0)
            dec_scale(B - 1, 0)
            z_stats(B - 1, 0)
            dec_stats(B - 1, 1)
            dec_scale(B - 1, 1)
            z_unit(B - 1, 0)
            z_stats(B - 1, 1)
            z_add(B - 1, 0)
            z_norm(B - 1, 1)


_INS = ["L0_attn_x", "L0_attn_Wq", "L0_attn_bq", "L0_attn_Wk", "L0_attn_bk", "L0_attn_Wv", "L0_attn_bv",
        "L0_ffn_W_enc", "L0_ffn_b_enc", "L0_ffn_W_s2c", "L0_ffn_b_s2c", "L0_ffn_Wr", "L0_ffn_br", "L0_ffn_W1",
        "L0_ffn_b1", "L0_ffn_W2", "L0_ffn_b2", "L0_ffn_W_c2s", "L0_ffn_b_c2s", "L0_ffn_W_dec", "L0_ffn_b_dec",
        "L0_ffn_ln_g", "L0_ffn_ln_b"]


def kernel(**inputs):
    import numpy as _np
    import concourse.bacc as _bacc
    from concourse import mybir as _mybir
    from concourse.bass_utils import run_bass_kernel_spmd as _run

    nc = _bacc.Bacc("TRN2", target_bir_lowering=False, num_devices=1)
    arrays, args = {}, []
    for name in _INS:
        a = _np.ascontiguousarray(inputs[name])
        arrays[f"in_{name}"] = a
        args.append(nc.dram_tensor(f"in_{name}", a.shape, _mybir.dt.from_np(a.dtype), kind="ExternalInput").ap())
    shape = tuple(inputs["L0_attn_x"].shape)
    args.append(nc.dram_tensor("out", shape, _mybir.dt.float32, kind="ExternalOutput").ap())
    attention_moe_block(nc, *args)
    r = _run(nc, [arrays], core_ids=[0])
    return r.results[0]["out"]
```
